# Optimizing a Trainium2 kernel written in Bass

```python
import numpy as np
import jax
import jax.numpy as jnp

def _softmax(x, axis=-1):
    return jax.nn.softmax(x, axis=axis)

def _gelu(x):
    return jax.nn.gelu(x, approximate=True)

def _silu(x):
    return jax.nn.silu(x)

def _sigmoid(x):
    return jax.nn.sigmoid(x)

def _layernorm(x, axis=-1, eps=1e-05):
    m = jnp.mean(x, axis=axis, keepdims=True)
    v = jnp.var(x, axis=axis, keepdims=True)
    return (x - m) / jnp.sqrt(v + eps)

def _scatter_add(tgt, idx, src, axis=0):
    return tgt.at[idx].add(src)

def _segment_sum(src, seg, n):
    return jax.ops.segment_sum(src, seg, n)
kernel_name = 'mk_cond_resid_d2_seqx_r4_178309'

def setup_inputs(seed: int=0):
    np.random.seed(seed)
    _w = jnp.asarray

    def _rec_inputs():
        import jax
        import jax.numpy as jnp
        _rk = jax.random.key(seed)
        x = 8.748e-05 + 1 * jax.random.normal(jax.random.fold_in(_rk, 1), (128, 64, 512), jnp.float32)
        _lenS = 64 - jax.random.randint(jax.random.fold_in(_rk, 7), (128,), 0, max(1, 64 // 4) + 1, jnp.int32)
        _lenS2 = 64 - jax.random.randint(jax.random.fold_in(_rk, 8), (128,), 0, max(1, 64 // 4) + 1, jnp.int32)
        cond_2048 = -9.80646e-05 + 1.00041 * jax.random.normal(jax.random.fold_in(_rk, 11), (128, 512), jnp.float32)
        return (x, cond_2048)
    x, cond_2048 = _rec_inputs()

    def _L0_cond_setup():
        import jax, jax.numpy as jnp
        import numpy as np
        DT = 0.01
        EPSILON = 0.08
        ALPHA = 0.7
        BETA = 0.8
        CLAMP = 20.0
        B, T, N = (64, 128, 512)

        def _derivative(q, p, drive, coupling, bias):
            i_couple = jnp.tanh(q) @ coupling.T
            dq = q - q ** 3 / 3.0 - p + drive + i_couple + bias
            dp = EPSILON * (q + ALPHA - BETA * p)
            return (dq, dp)

        def _rk4_step(q, p, drive, coupling, bias):
            dq1, dp1 = _derivative(q, p, drive, coupling, bias)
            dq2, dp2 = _derivative(q + 0.5 * DT * dq1, p + 0.5 * DT * dp1, drive, coupling, bias)
            dq3, dp3 = _derivative(q + 0.5 * DT * dq2, p + 0.5 * DT * dp2, drive, coupling, bias)
            dq4, dp4 = _derivative(q + DT * dq3, p + DT * dp3, drive, coupling, bias)
            q_next = q + DT / 6.0 * (dq1 + 2 * dq2 + 2 * dq3 + dq4)
            p_next = p + DT / 6.0 * (dp1 + 2 * dp2 + 2 * dp3 + dp4)
            q_next = jnp.clip(q_next, -CLAMP, CLAMP)
            p_next = jnp.clip(p_next, -CLAMP, CLAMP)
            return (q_next, p_next)
        key = jax.random.key(seed)
        k1, k2, k3, k4 = jax.random.split(key, 4)
        return {'q0': jax.random.normal(k1, (B, N), dtype=jnp.float32), 'p0': jax.random.normal(k2, (B, N), dtype=jnp.float32), 'input_drive_seq': jax.random.normal(k3, (B, T, N), dtype=jnp.float32), 'coupling': jax.random.normal(k4, (N, N), dtype=jnp.float32) * 0.01, 'bias': jnp.zeros((N,), dtype=jnp.float32)}
    _L0_cond_all = _L0_cond_setup()
    _L0_cond_in = {k: v for k, v in _L0_cond_all.items() if k in ('coupling', 'bias')}
    del _L0_cond_all

    def _L1_cond_setup():
        import jax, jax.numpy as jnp
        import numpy as np
        HEADS = 16
        EPS = 1e-06

        def _rms_norm(x, g):
            xf = x.astype(jnp.float32)
            y = xf * jax.lax.rsqrt(jnp.mean(xf * xf, axis=-1, keepdims=True) + EPS)
            return y.astype(x.dtype) * g
        key = jax.random.key(seed)
        ks = jax.random.split(key, 6)
        b, n, dim, emb_dim = (4, 512, 512, 512)
        d_head = dim // HEADS
        return {'x': jax.random.normal(ks[0], (b, n, dim), jnp.float32), 'emb': jax.random.normal(ks[1], (b, 1, emb_dim), jnp.float32), 'W_emb': jax.random.normal(ks[2], (emb_dim, 2 * dim), jnp.float32) * emb_dim ** (-0.5), 'b_emb': jnp.zeros((2 * dim,), jnp.float32), 'g_norm': jnp.ones((dim,), jnp.float32), 'W_qkv': jax.random.normal(ks[3], (dim, 3 * dim), jnp.float32) * dim ** (-0.5), 'g_q': jnp.ones((d_head,), jnp.float32), 'g_k': jnp.ones((d_head,), jnp.float32), 'W_out': jax.random.normal(ks[4], (dim, dim), jnp.float32) * dim ** (-0.5)}
    _L1_cond_all = _L1_cond_setup()
    _L1_cond_in = {k: v for k, v in _L1_cond_all.items() if k in ('W_emb', 'b_emb', 'g_norm', 'W_qkv', 'g_q', 'g_k', 'W_out')}
    del _L1_cond_all
    return {'x': x, 'cond_2048': cond_2048, 'L0_cond_coupling': _L0_cond_in['coupling'], 'L0_cond_bias': _L0_cond_in['bias'], 'L1_cond_W_emb': _L1_cond_in['W_emb'], 'L1_cond_b_emb': _L1_cond_in['b_emb'], 'L1_cond_g_norm': _L1_cond_in['g_norm'], 'L1_cond_W_qkv': _L1_cond_in['W_qkv'], 'L1_cond_g_q': _L1_cond_in['g_q'], 'L1_cond_g_k': _L1_cond_in['g_k'], 'L1_cond_W_out': _L1_cond_in['W_out']}

def reference(x, cond_2048, L0_cond_coupling, L0_cond_bias, L1_cond_W_emb, L1_cond_b_emb, L1_cond_g_norm, L1_cond_W_qkv, L1_cond_g_q, L1_cond_g_k, L1_cond_W_out):
    import jax
    import jax.numpy as jnp

    def _L0_cond_ref(q0, p0, input_drive_seq, coupling, bias):
        import jax, jax.numpy as jnp
        import numpy as np
        DT = 0.01
        EPSILON = 0.08
        ALPHA = 0.7
        BETA = 0.8
        CLAMP = 20.0
        B, T, N = (64, 128, 512)

        def _derivative(q, p, drive, coupling, bias):
            i_couple = jnp.tanh(q) @ coupling.T
            dq = q - q ** 3 / 3.0 - p + drive + i_couple + bias
            dp = EPSILON * (q + ALPHA - BETA * p)
            return (dq, dp)

        def _rk4_step(q, p, drive, coupling, bias):
            dq1, dp1 = _derivative(q, p, drive, coupling, bias)
            dq2, dp2 = _derivative(q + 0.5 * DT * dq1, p + 0.5 * DT * dp1, drive, coupling, bias)
            dq3, dp3 = _derivative(q + 0.5 * DT * dq2, p + 0.5 * DT * dp2, drive, coupling, bias)
            dq4, dp4 = _derivative(q + DT * dq3, p + DT * dp3, drive, coupling, bias)
            q_next = q + DT / 6.0 * (dq1 + 2 * dq2 + 2 * dq3 + dq4)
            p_next = p + DT / 6.0 * (dp1 + 2 * dp2 + 2 * dp3 + dp4)
            q_next = jnp.clip(q_next, -CLAMP, CLAMP)
            p_next = jnp.clip(p_next, -CLAMP, CLAMP)
            return (q_next, p_next)
        drive_tbn = jnp.swapaxes(input_drive_seq, 0, 1)

        def scan_fn(carry, drive):
            q, p = carry
            q, p = _rk4_step(q, p, drive, coupling, bias)
            return ((q, p), q)
        (_, _), q_trace_tbn = jax.lax.scan(scan_fn, (q0, p0), drive_tbn)
        return jnp.swapaxes(q_trace_tbn, 0, 1)

    def _L1_cond_ref(x, emb, W_emb, b_emb, g_norm, W_qkv, g_q, g_k, W_out):
        import jax, jax.numpy as jnp
        import numpy as np
        HEADS = 16
        EPS = 1e-06

        def _rms_norm(x, g):
            xf = x.astype(jnp.float32)
            y = xf * jax.lax.rsqrt(jnp.mean(xf * xf, axis=-1, keepdims=True) + EPS)
            return y.astype(x.dtype) * g
        b, n, dim = x.shape
        h = HEADS
        d = dim // h
        scale_shift = emb @ W_emb + b_emb
        scale, shift = jnp.split(scale_shift, 2, axis=-1)
        xn = _rms_norm(x, g_norm) * (1.0 + scale) + shift
        qkv = xn @ W_qkv
        qkv = qkv.reshape(b, n, 3, h, d)
        q, k, v = jnp.moveaxis(qkv, 2, 0)
        q = jnp.swapaxes(q, 1, 2)
        k = jnp.swapaxes(k, 1, 2)
        v = jnp.swapaxes(v, 1, 2)
        q = _rms_norm(q, g_q)
        k = _rms_norm(k, g_k)
        logits = jnp.einsum('bhqd,bhkd->bhqk', q, k) * d ** (-0.5)
        attn = jax.nn.softmax(logits, axis=-1)
        o = jnp.einsum('bhqk,bhkd->bhqd', attn, v)
        o = jnp.swapaxes(o, 1, 2).reshape(b, n, dim)
        return o + o @ W_out
    x = x + _L0_cond_ref(cond_2048, cond_2048, x, L0_cond_coupling, L0_cond_bias)
    x = x + _L1_cond_ref(x, cond_2048[:, None, :], L1_cond_W_emb, L1_cond_b_emb, L1_cond_g_norm, L1_cond_W_qkv, L1_cond_g_q, L1_cond_g_k, L1_cond_W_out)
    return x

_drawn_inputs = setup_inputs


def setup_inputs(seed=0):
    import zlib

    import numpy as np

    out = dict(_drawn_inputs(seed))
    spreads = {'L0_cond_bias': (0.0, 0.1),
     'L1_cond_b_emb': (0.0, 0.1),
     'L1_cond_g_norm': (1.0, 0.2),
     'L1_cond_g_q': (1.0, 0.6),
     'L1_cond_g_k': (1.0, 0.6)}
    factors = {}
    for name, (base, spread) in spreads.items():
        noise = np.random.default_rng([zlib.crc32(name.encode()), seed]).standard_normal(out[name].shape)
        drawn = base * np.exp(spread * noise) if base else spread * noise
        out[name] = jnp.asarray(drawn.astype(out[name].dtype))
    for name, factor in factors.items():
        out[name] = (out[name] * factor).astype(out[name].dtype)
    return out
```

```python
from contextlib import ExitStack

import numpy as np

import concourse.bass as bass
from concourse import mybir

F32 = mybir.dt.float32
F32R = mybir.dt.float32r
I32 = mybir.dt.int32
ALU = mybir.AluOpType
ACT = mybir.ActivationFunctionType
AX = mybir.AxisListType

P = 128
DT, EPSILON, ALPHA, BETA, CLAMP = 0.01, 0.08, 0.7, 0.8, 20.0
HEADS, EPS = 16, 1e-6
STAGES = 4
P_SHIFT = ALPHA / BETA


def rk4_weights():
    q1, q2, q3, q4, p, drive = np.eye(6)
    half = 0.5 * DT

    def dp(q, p_stage):
        return EPSILON * (q - BETA * p_stage)

    p2 = p + half * dp(q1, p)
    p3 = p + half * dp(q2, p2)
    p4 = p + DT * dp(q3, p3)
    p_next = p + DT / 6.0 * (dp(q1, p) + 2 * dp(q2, p2) + 2 * dp(q3, p3) + dp(q4, p4))
    base = [
        q1 + half * (drive - p),
        q1 + half * (drive - p2),
        q1 + DT * (drive - p3),
        (q2 + 2 * q3 + q4 - q1) / 3.0 + DT / 6.0 * (drive - p4),
    ]
    step = [half, half, DT, DT / 6.0]
    return step, [[float(v) for v in b] for b in base], [float(v) for v in p_next]


def fhn_attention_kernel(nc, x, cond, coupling, bias, w_emb, b_emb, g_norm, w_qkv, g_q, g_k, w_out, out):
    B, T, N = x.shape
    C = N // P
    D = N // HEADS
    HG = P // D
    G = HEADS // HG
    HP = HEADS // 2
    PAIRS = B * T // P
    assert B == P and 2 * T == P and C * P == N and G == C
    A_STEP, BASE, P_NEXT = rk4_weights()
    Q1, Q2, Q3, Q4, PP, DR = range(6)
    COMBOS = 11

    x1_scratch = nc.dram_tensor("x1_scratch", (B, T, N), F32, kind="Internal").ap()
    qk_scratch = nc.dram_tensor("qk_scratch", (B, T, 2 * N), F32, kind="Internal").ap()
    v_scratch = nc.dram_tensor("v_scratch", (B, 2, T, N), F32, kind="Internal").ap()

    with ExitStack() as ctx:
        def sb(name, shape, dt=F32):
            return ctx.enter_context(nc.sbuf_tensor(name, shape, dt))

        def sem(name):
            return ctx.enter_context(nc.semaphore(name))

        psum = ctx.enter_context(nc.psum_tensor("psum", [P, 8, 512], F32))
        ps_couple, ps_qT, ps_cube, ps_tanh, ps_xnT = (psum[:, n, :] for n in range(5))
        ps_qkv = [psum[:, 5 + n, :] for n in range(3)]
        ps_QT, ps_KT, ps_O, ps_Y = psum[:, 0, :], psum[:, 1, :], psum[:, 6, :], psum[:, 7, :]
        ps_S = psum[:, 2:4, :].rearrange("p a n -> p (a n)")
        ps_PT = psum[:, 4:6, :].rearrange("p a n -> p (a n)")

        ident = sb("ident", [P, P])
        bias_row = sb("bias_row", [P, N])
        gs_row = sb("gs_row", [P, N])
        shift_row = sb("shift_row", [P, N])
        emb_bias = sb("emb_bias", [P, 2 * N])
        gq_col = sb("gq_col", [P, 1])
        gk_col = sb("gk_col", [P, 1])
        gqk_col = sb("gqk_col", [P, 1])
        condT = sb("condT", [P, C, P])
        stage_w = sb("stage_w", [P, C, 3 * N])
        wout_f32 = sb("wout_f32", [P, C, N])
        couple_hi = sb("couple_hi", [P, C, N], F32R)
        couple_lo = sb("couple_lo", [P, C, N], F32R)
        wqkv_hi = sb("wqkv_hi", [P, C, 3 * N], F32R)
        wqkv_lo = sb("wqkv_lo", [P, C, 3 * N], F32R)
        wout_hi = sb("wout_hi", [P, C, N], F32R)
        wout_lo = sb("wout_lo", [P, C, N], F32R)

        q = [sb(f"q{s + 1}", [P, N]) for s in range(STAGES)]
        p_state = sb("p_state", [P, N])
        p_sum = sb("p_sum", [P, N])
        qraw = sb("qraw", [P, N])
        b_term = sb("b_term", [P, N])
        tanh_hi = sb("tanh_hi", [P, N], F32R)
        tanh_lo = sb("tanh_lo", [P, N], F32R)
        x_in = [sb(f"x_in{k}", [P, N]) for k in range(2)]
        drive = sb("drive", [P, N])
        drive_s = [sb(f"drive_s{n}", [P, N]) for n in range(3)]
        p_s = [sb(f"p_s{s}", [P, N]) for s in range(STAGES)]
        q1_s = [sb(f"q1_s{s}", [P, N]) for s in range(1, STAGES)]
        base_all = sb("base_all", [P, STAGES * N])
        base = [base_all[:, s * N:(s + 1) * N] for s in range(STAGES)]
        x1 = sb("x1", [P, N])
        sq_dump = condT[:, :, :].rearrange("p c n -> p (c n)")
        sumsq = sb("sumsq", [P, 1])
        sumsq_eps = sb("sumsq_eps", [P, 1])
        minus_half = sb("minus_half", [P, 1])
        eps_col = sb("eps_col", [P, 1])
        rms = sb("rms", [P, 1])
        xg = sb("xg", [P, N])
        xn = sb("xn", [P, N])
        xnT_hi = sb("xnT_hi", [P, C, P], F32R)
        xnT_lo = sb("xnT_lo", [P, C, P], F32R)
        head_sq = sb("head_sq", [P, N])
        head_sum = sb("head_sum", [P, 2 * HEADS])
        head_eps = sb("head_eps", [P, 2 * HEADS])
        head_half = sb("head_half", [P, 2 * HEADS])
        head_rms = sb("head_rms", [P, 2 * HEADS])
        head_tmp = sb("head_tmp", [P, 2 * HEADS])
        qk_row = sb("qk_row", [P, 2 * N])
        v_row = sb("v_row", [P, 2, N])

        staged = stage_w[:, :, :].rearrange("p c n -> p (c n)")
        staged_out = wout_f32[:, :, :].rearrange("p c n -> p (c n)")
        qk_in = [staged[:, 2 * k * N:2 * (k + 1) * N] for k in range(2)]
        v_in = [staged[:, (4 + 2 * k) * N:(6 + 2 * k) * N].rearrange("p (b n) -> p b n", b=2) for k in range(2)]
        KT_diag = staged[:, 8 * N:12 * N].rearrange("p (g b h k) -> p g b h k", g=G, b=2, h=HG)
        PT = base_all[:, 0:2 * N].rearrange("p (h n) -> p h n", h=HP)
        shifted = base_all[:, 2 * N:4 * N].rearrange("p (h k) -> p h k", h=HEADS)
        probs = staged_out[:, 0:2 * N].rearrange("p (h k) -> p h k", h=HEADS)
        y_row = [staged_out[:, (2 + k) * N:(3 + k) * N] for k in range(2)]
        x1_in = [sb(f"x1_in{k}", [P, N]) for k in range(2)]
        QT = sb("QT", [P, G, P])
        neg_max = sb("neg_max", [P, HEADS])
        row_sum = sb("row_sum", [P, HEADS])
        row_rcp = sb("row_rcp", [P, HEADS])
        o_row, resid, oT_hi, oT_lo = xn, xg, xnT_hi, xnT_lo

        cond_in, couple_in, wqkv_in, wout_in, wemb_in, rows_in, gcols_in = (
            sem(n) for n in ("cond_in", "couple_in", "wqkv_in", "wout_in", "wemb_in", "rows_in", "gcols_in"))
        ident_zero, ident_ready, zeros_ready = sem("ident_zero"), sem("ident_ready"), sem("zeros_ready")
        coupT_ready, coup_hi_ready, coup_split = sem("coupT_ready"), sem("coup_hi_ready"), sem("coup_split")
        condT_done, condT_copied = sem("condT_done"), sem("condT_copied")
        emb_done, emb_read, emb_step = sem("emb_done"), sem("emb_read"), sem("emb_step")
        wqkv_hi_ready, wqkv_split = sem("wqkv_hi_ready"), sem("wqkv_split")
        wout_hi_ready, wout_split = sem("wout_hi_ready"), sem("wout_split")
        bias_ready, gqk_ready, gqk_step = sem("bias_ready"), sem("gqk_ready"), sem("gqk_step")
        q_ready, qT_ready, tanh_hi_ready, tanh_ready, tanh_lo_ready, coupled = (
            sem(n) for n in ("q_ready", "qT_ready", "tanh_hi_ready", "tanh_ready", "tanh_lo_ready", "coupled"))
        sq_ready, cube_ready, b_ready, combos = sem("sq_ready"), sem("cube_ready"), sem("b_ready"), sem("combos")
        drive_ready, drive_s_ready, p_s_ready, q1_s_ready = (
            sem(n) for n in ("drive_ready", "drive_s_ready", "p_s_ready", "q1_s_ready"))
        pd_ready, base_ready = sem("pd_ready"), sem("base_ready")
        x_loaded = [sem(f"x_loaded{k}") for k in range(2)]
        x1_ready, x1_stored, sumsq_ready, rms_ready, xg_ready, xn_ready, xnT_ready = (
            sem(n) for n in ("x1_ready", "x1_stored", "sumsq_ready", "rms_ready", "xg_ready", "xn_ready", "xnT_ready"))
        xnT_hi_ready, xnT_lo_ready, qkv_done = sem("xnT_hi_ready"), sem("xnT_lo_ready"), sem("qkv_done")
        head_sq_ready, head_sum_ready, head_rms_ready, qk_ready, v_ready = (
            sem(n) for n in ("head_sq_ready", "head_sum_ready", "head_rms_ready", "qk_ready", "v_ready"))
        half_ready, sumsq_eps_ready = sem("half_ready"), sem("sumsq_eps_ready")
        qk_stored, v_stored = sem("qk_stored"), sem("v_stored")
        qk_loaded, v_loaded, x1_loaded, y_stored = (
            [sem(f"{n}{k}") for k in range(2)] for n in ("qk_loaded", "v_loaded", "x1_loaded", "y_stored"))
        QKT_ready, QT_copied, KT_copied, S_ready, max_ready, shifted_ready, probs_ready = (
            sem(n) for n in ("QKT_ready", "QT_copied", "KT_copied", "S_ready", "max_ready", "shifted_ready", "probs_ready"))
        sum_ready, rcp_ready, PT_ready, PT_copied, O_ready, o_ready, oT_ready = (
            sem(n) for n in ("sum_ready", "rcp_ready", "PT_ready", "PT_copied", "O_ready", "o_ready", "oT_ready"))
        oT_hi_ready, oT_lo_ready, Y_ready, resid_ready, y_ready = (
            sem(n) for n in ("oT_hi_ready", "oT_lo_ready", "Y_ready", "resid_ready", "y_ready"))

        coupling_nat = stage_w[:, :, 0:N]
        wemb_nat = stage_w[:, :, N:3 * N]
        wqkv_nat = stage_w[:, :, :]

        def rows(t):
            return bass.ds(t, 1)

        block = ctx.enter_context(nc.Block())

        @block.sync
        def _(sp):
            sp.dma_start(coupling_nat, coupling.rearrange("(c n) m -> n c m", c=C)).then_inc(couple_in, 16)
            sp.dma_start(q[1][:, :], cond).then_inc(cond_in, 16)
            sp.dma_start(x_in[0][:, :], x[:, 0, :]).then_inc(x_loaded[0], 16)
            sp.dma_start(x_in[1][:, :], x[:, 1, :]).then_inc(x_loaded[1], 16)
            sp.dma_start(bias_row[:, :], bias.partition_broadcast(P)).then_inc(rows_in, 16)
            sp.dma_start(gs_row[:, :], g_norm.partition_broadcast(P)).then_inc(rows_in, 16)
            sp.dma_start(emb_bias[:, :], b_emb.partition_broadcast(P)).then_inc(rows_in, 16)
            sp.dma_start(wemb_nat, w_emb.rearrange("(c p) n -> p c n", c=C)).then_inc(wemb_in, 16)
            sp.dma_start(wout_f32[:, :, :], w_out.rearrange("(c p) n -> p c n", c=C)).then_inc(wout_in, 16)
            for h in range(HG):
                sp.dma_start(gq_col[h * D:(h + 1) * D, :], g_q.unsqueeze(1)).then_inc(gcols_in, 16)
                sp.dma_start(gk_col[h * D:(h + 1) * D, :], g_k.unsqueeze(1)).then_inc(gcols_in, 16)
            sp.wait_ge(coupT_ready, C)
            sp.wait_ge(emb_done, 2)
            sp.dma_start(wqkv_nat, w_qkv.rearrange("(c p) n -> p c n", c=C)).then_inc(wqkv_in, 16)

            def load_x(t, k, m):
                sp.wait_ge(x1_ready, t - 1)
                sp.dma_start(x_in[k][:, :], x[:, rows(t), :].rearrange("b o n -> b (o n)")).then_inc(x_loaded[k], 16)

            def store_x1(t):
                sp.wait_ge(x1_ready, t + 1)
                sp.dma_start(x1_scratch[:, rows(t), :].rearrange("b o n -> b (o n)"), x1[:, :]).then_inc(x1_stored, 16)

            def store_qkv(t):
                sp.wait_ge(qk_ready, t + 1)
                sp.dma_start(qk_scratch[:, rows(t), :].rearrange("b o n -> b (o n)"), qk_row[:, :]).then_inc(qk_stored, 16)
                sp.wait_ge(v_ready, t + 1)
                sp.dma_start(v_scratch[:, :, rows(t), :].rearrange("b e o n -> b e (o n)"), v_row[:, :, :]).then_inc(v_stored, 16)

            load_x(2, 0, 1)
            store_x1(0)
            with sp.Fori(1, T // 2) as m:
                for k in range(2):
                    t = m * 2 + k
                    if k == 0:
                        load_x(t + 1, 1, m)
                        store_x1(t - 1)
                    else:
                        store_x1(t - 1)
                        sp.wait_ge(x1_ready, t)
                        nxt = (t + 1) % T
                        sp.dma_start(x_in[0][:, :], x[:, rows(nxt), :].rearrange("b o n -> b (o n)")).then_inc(x_loaded[0], 16)
                    store_qkv(t - 2)
            store_qkv(T - 2)
            store_x1(T - 1)
            store_qkv(T - 1)

            sp.wait_ge(x_loaded[0], 16 * (T // 2 + 1))
            sp.wait_ge(qk_stored, 16 * T)
            sp.wait_ge(v_stored, 16 * T)
            sp.wait_ge(x1_stored, 16 * T)
            x1_tok = x1_scratch.rearrange("(i b) t n -> i (b t) n", b=2)
            qk_tok = qk_scratch.rearrange("(i b) t n -> i (b t) n", b=2)
            v_tok = v_scratch.rearrange("(i b) e t n -> i (e t) b n", b=2)
            y_tok = out.rearrange("(i b) t n -> i (b t) n", b=2)

            def tile_of(a, i):
                return a[bass.ds(i, 1)]

            def load_qk(i, k):
                sp.dma_start(qk_in[k], tile_of(qk_tok, i).rearrange("o p n -> (o p) n")).then_inc(qk_loaded[k], 16)

            def load_vx(i, k):
                sp.dma_start(v_in[k], tile_of(v_tok, i).rearrange("o p b n -> (o p) b n")).then_inc(v_loaded[k], 16)
                sp.dma_start(x1_in[k][:, :], tile_of(x1_tok, i).rearrange("o p n -> (o p) n")).then_inc(x1_loaded[k], 16)

            def store_y(i, k):
                sp.wait_ge(y_ready, i + 1)
                sp.dma_start(tile_of(y_tok, i).rearrange("o p n -> (o p) n"), y_row[k]).then_inc(y_stored[k], 16)

            load_qk(0, 0)
            load_qk(1, 1)
            load_vx(0, 0)
            sp.wait_ge(QKT_ready, 1)
            load_qk(2, 0)

            def steady(i, k, qk, store):
                if qk:
                    sp.wait_ge(QKT_ready, i + 2)
                    load_qk(i + 3, 1 - k)
                if store:
                    sp.wait_ge(O_ready, i)
                    sp.wait_ge(resid_ready, i)
                load_vx(i + 1, 1 - k)
                if store:
                    store_y(i - 1, 1 - k)

            steady(0, 0, True, False)
            steady(1, 1, True, True)
            with sp.Fori(1, PAIRS // 2 - 2) as m:
                for k in range(2):
                    steady(m * 2 + k, k, True, True)
            steady(PAIRS - 4, 0, True, True)
            steady(PAIRS - 3, 1, False, True)
            steady(PAIRS - 2, 0, False, True)
            store_y(PAIRS - 2, 0)
            store_y(PAIRS - 1, 1)
            for k in range(2):
                sp.wait_ge(y_stored[k], 16 * (PAIRS // 2))

        @block.tensor
        def _(pe):
            def couple(n):
                for c in range(C):
                    if c == 0:
                        pe.wait_ge(tanh_hi_ready, n + 1)
                    pe.matmul(ps_couple, tanh_hi[:, c * P:(c + 1) * P], couple_hi[:, c, :], start=(c == 0), stop=False)
                for c in range(C):
                    pe.matmul(ps_couple, tanh_hi[:, c * P:(c + 1) * P], couple_lo[:, c, :], start=False, stop=False)
                for c in range(C):
                    if c == 0:
                        pe.wait_ge(tanh_lo_ready, n + 1)
                    mm = pe.matmul(ps_couple, tanh_lo[:, c * P:(c + 1) * P], couple_hi[:, c, :], start=False, stop=(c == C - 1))
                mm.then_inc(coupled, 1)

            def transpose_q(n, src):
                pe.wait_ge(q_ready, n + 1)
                for c in range(C):
                    mm = pe.transpose(ps_qT[:, c * P:(c + 1) * P], src[:, c * P:(c + 1) * P], ident[:, :])
                mm.then_inc(qT_ready, 1)

            PRODUCTS = [(a, w, c) for a, w in ((xnT_hi, wqkv_hi), (xnT_hi, wqkv_lo), (xnT_lo, wqkv_hi)) for c in range(C)]

            def project(t, lo, hi):
                for j in range(lo, hi):
                    part, r = divmod(j, len(PRODUCTS))
                    a, w, c = PRODUCTS[r]
                    if j == 0:
                        pe.wait_ge(xnT_lo_ready, t + 1)
                        if not (isinstance(t, int) and t == 0):
                            pe.wait_ge(qk_ready, t)
                    if r == 0 and part == 2 and not (isinstance(t, int) and t == 0):
                        pe.wait_ge(v_ready, t)
                    mm = pe.matmul(ps_qkv[part], a[:, c, :], w[:, c, part * N:(part + 1) * N],
                                   start=(r == 0), stop=(r == len(PRODUCTS) - 1))
                    if r == len(PRODUCTS) - 1:
                        mm.then_inc(qkv_done, 1)

            def transpose_xn(t):
                pe.wait_ge(xn_ready, t + 1)
                for c in range(C):
                    mm = pe.transpose(ps_xnT[:, c * P:(c + 1) * P], xn[:, c * P:(c + 1) * P], ident[:, :])
                mm.then_inc(xnT_ready, 1)

            pe.wait_ge(ident_ready, 1)
            pe.wait_ge(couple_in, 16)
            for c in range(C):
                for g in range(C):
                    mm = pe.transpose(psum[:, c, g * P:(g + 1) * P], coupling_nat[:, g, c * P:(c + 1) * P], ident[:, :])
                mm.then_inc(coupT_ready, 1)
            pe.wait_ge(cond_in, 16)
            for c in range(C):
                mm = pe.transpose(psum[:, 4, c * P:(c + 1) * P], q[1][:, c * P:(c + 1) * P], ident[:, :])
            mm.then_inc(condT_done, 1)
            pe.wait_ge(wemb_in, 16)
            pe.wait_ge(condT_copied, 1)
            for half in range(2):
                for c in range(C):
                    mm = pe.matmul(psum[:, 5 + half, :], condT[:, c, :], wemb_nat[:, c, half * N:(half + 1) * N],
                                   start=(c == 0), stop=(c == C - 1))
                mm.then_inc(emb_done, 1)
            pe.wait_ge(coup_split, C)
            transpose_q(0, q[0])

            def step(t, stages_ahead, fill_two, fill_one):
                n = t * STAGES
                for s in range(STAGES):
                    couple(n + s)
                    old = fill_two and s < 2
                    new = fill_one and s >= 2
                    lo = 18 + 9 * s if old else 9 * (s - 2)
                    tt = t - 2 if old else t - 1
                    if old or new:
                        project(tt, lo, lo + 4)
                    if s < STAGES - 1 or stages_ahead:
                        transpose_q(n + s + 1, q[(s + 1) % STAGES])
                    if old or new:
                        project(tt, lo + 4, lo + 9)
                    if s == 1 and fill_one:
                        transpose_xn(t - 1)

            pe.wait_ge(emb_read, 2)
            step(0, True, False, False)
            pe.wait_ge(wqkv_split, 1)
            step(1, True, False, True)
            with pe.Fori(1, T // 2 - 1) as m:
                for k in range(2):
                    step(m * 2 + k, True, True, True)
            step(T - 2, True, True, True)
            step(T - 1, False, True, True)
            project(T - 2, 18, 36)
            transpose_xn(T - 1)
            project(T - 1, 0, 36)

            def transpose_qk(i, k, m):
                pe.wait_ge(qk_loaded[k], 16 * m + 16)
                for g in range(G):
                    pe.transpose(ps_QT[:, g * P:(g + 1) * P], qk_in[k][:, g * P:(g + 1) * P], ident[:, :])
                for g in range(G):
                    mm = pe.transpose(ps_KT[:, g * P:(g + 1) * P], qk_in[k][:, N + g * P:N + (g + 1) * P], ident[:, :])
                mm.then_inc(QKT_ready, 1)

            def scores(i):
                pe.wait_ge(QT_copied, i + 1)
                pe.wait_ge(KT_copied, i + 1)
                for g in range(G):
                    for b in range(2):
                        mm = pe.matmul(ps_S[b * T:(b + 1) * T, g * HG * T:(g + 1) * HG * T],
                                       QT[:, g, b * T:(b + 1) * T],
                                       KT_diag[:, g, b, :, :].rearrange("p h k -> p (h k)"), start=True, stop=True)
                mm.then_inc(S_ready, 1)

            def transpose_probs(i):
                pe.wait_ge(probs_ready, i + 1)
                for hp in range(HP):
                    mm = pe.transpose(ps_PT[:, hp * P:(hp + 1) * P],
                                      probs[:, 2 * hp:2 * hp + 2, :].rearrange("p h k -> p (h k)"), ident[:, :])
                mm.then_inc(PT_ready, 1)

            def attend(i, k, m):
                pe.wait_ge(PT_copied, i + 1)
                pe.wait_ge(v_loaded[k], 16 * m + 16)
                for hp in range(HP):
                    for b in range(2):
                        mm = pe.matmul(ps_O[b * T:(b + 1) * T, hp * 2 * D:(hp + 1) * 2 * D],
                                       PT[:, hp, b * T:(b + 1) * T], v_in[k][:, b, hp * 2 * D:(hp + 1) * 2 * D],
                                       start=True, stop=True)
                mm.then_inc(O_ready, 1)

            def transpose_o(i):
                pe.wait_ge(o_ready, i + 1)
                for c in range(C):
                    mm = pe.transpose(ps_O[:, c * P:(c + 1) * P], o_row[:, c * P:(c + 1) * P], ident[:, :])
                mm.then_inc(oT_ready, 1)

            def project_out(i, first):
                if not first:
                    pe.wait_ge(y_ready, i)
                for j, (a, w) in enumerate(((oT_hi, wout_hi), (oT_hi, wout_lo), (oT_lo, wout_hi))):
                    if j == 0:
                        pe.wait_ge(oT_hi_ready, i + 1)
                    if j == 2:
                        pe.wait_ge(oT_lo_ready, i + 1)
                    for c in range(C):
                        mm = pe.matmul(ps_Y, a[:, c, :], w[:, c, :], start=(j == 0 and c == 0), stop=(j == 2 and c == C - 1))
                mm.then_inc(Y_ready, 1)

            def pair(i, k, m, first=False, score=True, qk=True):
                if score:
                    scores(i + 1)
                attend(i, k, m)
                if qk:
                    transpose_qk(i + 2, k, m + 1)
                transpose_o(i)
                if score:
                    transpose_probs(i + 1)
                project_out(i, first)

            pe.wait_ge(qk_ready, T)
            pe.wait_ge(v_ready, T)
            transpose_qk(0, 0, 0)
            scores(0)
            transpose_qk(1, 1, 0)
            transpose_probs(0)
            pe.wait_ge(wout_split, 1)
            pair(0, 0, 0, first=True)
            pair(1, 1, 0)
            with pe.Fori(1, PAIRS // 2 - 1) as m:
                for k in range(2):
                    pair(m * 2 + k, k, m)
            pair(PAIRS - 2, 0, PAIRS // 2 - 1, qk=False)
            pair(PAIRS - 1, 1, PAIRS // 2 - 1, score=False, qk=False)

        @block.scalar
        def _(act):
            def square_q(n, src):
                act.wait_ge(q_ready, n + 1)
                act.activation(ps_cube, src, ACT.Square).then_inc(sq_ready, 1)

            def tanh(n):
                act.wait_ge(qT_ready, n + 1)
                act.activation(tanh_hi[:, :], ps_qT, ACT.Tanh).then_inc(tanh_hi_ready, 1)
                act.activation(ps_tanh, ps_qT, ACT.Tanh).then_inc(tanh_ready, 1)

            def scale_drive(t, first=False):
                act.wait_ge(drive_ready, t + 1)
                if not first:
                    act.wait_ge(pd_ready, 4 * t)
                for n, f in enumerate((BASE[0][DR], BASE[2][DR], BASE[3][DR])):
                    o = act.activation(drive_s[n][:, :], drive[:, :], ACT.Copy, scale=f)
                o.then_inc(drive_s_ready, 1)

            def scale_p(t, first=False):
                act.wait_ge(combos, COMBOS * t - 1 if not first else 1)
                if not first:
                    act.wait_ge(pd_ready, 4 * t)
                for s in range(STAGES):
                    act.activation(p_s[s][:, :], p_state[:, :], ACT.Copy, scale=BASE[s][PP]).then_inc(p_s_ready, 1)

            def scale_q1(t, first=False):
                if not first:
                    act.wait_ge(base_ready, 4 * t)
                for s in range(1, STAGES):
                    act.activation(q1_s[s - 1][:, :], q[0][:, :], ACT.Copy, scale=BASE[s][Q1]).then_inc(q1_s_ready, 1)

            def square_x1(t):
                act.wait_ge(x1_ready, t + 1)
                act.activation(sq_dump, x1[:, :], ACT.Square, accum_out=sumsq[:, :]).then_inc(sumsq_ready, 1)

            def square_heads(t, part, first=False):
                act.wait_ge(qkv_done, 3 * t + part + 1)
                if not first:
                    act.wait_ge(head_sum_ready, 2 * t + part)
                act.activation(head_sq[:, :], ps_qkv[part], ACT.Square).then_inc(head_sq_ready, 1)

            def split_xnT(t):
                act.wait_ge(xnT_ready, t + 1)
                act.activation(xnT_hi[:, :, :].rearrange("p c n -> p (c n)"), ps_xnT, ACT.Copy).then_inc(xnT_hi_ready, 1)

            def copy_v(t, first=False):
                act.wait_ge(qkv_done, 3 * t + 3)
                if not first:
                    act.wait_ge(v_stored, 16 * t)
                else:
                    act.wait_ge(zeros_ready, 1)
                v = ps_qkv[2].rearrange("p (h e d) -> p h e d", e=2, d=D)
                for e in range(2):
                    o = act.activation(v_row[:, e, :].rearrange("p (h e d) -> p h e d", e=2, d=D)[:, :, e, :],
                                       v[:, :, e, :], ACT.Copy)
                o.then_inc(v_ready, 1)

            for c in range(C):
                act.wait_ge(coupT_ready, c + 1)
                act.activation(couple_hi[:, c, :], psum[:, c, :], ACT.Copy).then_inc(coup_hi_ready, 1)
            act.wait_ge(condT_done, 1)
            act.activation(condT[:, :, :].rearrange("p c n -> p (c n)"), psum[:, 4, :], ACT.Copy).then_inc(condT_copied, 1)
            act.wait_ge(coup_split, C)
            scale_p(0, first=True)
            scale_drive(0, first=True)

            def step(t, last, fill_two, fill_one, two_first=False, first=False):
                n = t * STAGES
                square_q(n, q[0][:, :])
                tanh(n)
                scale_q1(t, first)
                if fill_two:
                    square_heads(t - 2, 0, two_first)
                if fill_one:
                    square_x1(t - 1)
                square_q(n + 1, q[1][:, :])
                tanh(n + 1)
                if fill_two:
                    square_heads(t - 2, 1)
                square_q(n + 2, q[2][:, :])
                tanh(n + 2)
                if fill_one:
                    split_xnT(t - 1)
                if not last:
                    scale_drive(t + 1)
                if fill_two:
                    copy_v(t - 2, two_first)
                square_q(n + 3, q[3][:, :])
                tanh(n + 3)
                if not last:
                    scale_p(t + 1)

            step(0, False, False, False, first=True)
            act.wait_ge(wqkv_in, 16)
            for c in range(C):
                for part in range(3):
                    o = act.activation(wqkv_hi[:, c, part * N:(part + 1) * N], wqkv_nat[:, c, part * N:(part + 1) * N], ACT.Copy)
                o.then_inc(wqkv_hi_ready, 1)
            step(1, False, False, True)
            act.wait_ge(wout_in, 16)
            for c in range(C):
                o = act.activation(wout_hi[:, c, :], wout_f32[:, c, :], ACT.Copy)
            o.then_inc(wout_hi_ready, 1)
            step(2, False, True, True, two_first=True)
            step(3, False, True, True)
            with act.Fori(2, T // 2 - 1) as m:
                for k in range(2):
                    step(m * 2 + k, False, True, True)
            step(T - 2, False, True, True)
            step(T - 1, True, True, True)
            square_heads(T - 2, 0)
            square_x1(T - 1)
            square_heads(T - 2, 1)
            copy_v(T - 2)
            split_xnT(T - 1)
            square_heads(T - 1, 0)
            square_heads(T - 1, 1)
            copy_v(T - 1)

            def copy_KT(i):
                act.wait_ge(QKT_ready, i + 1)
                for h in range(HG):
                    r = slice(h * D, (h + 1) * D)
                    o = act.activation(KT_diag[r, :, :, h, :], ps_KT[r, :].rearrange("p (g b k) -> p g b k", g=G, b=2), ACT.Copy)
                o.then_inc(KT_copied, 1)

            def exp(i, first=False):
                act.wait_ge(shifted_ready, i + 1)
                if not first:
                    act.wait_ge(PT_ready, i)
                    act.wait_ge(sum_ready, i)
                act.activation(probs[:, :, :], shifted[:, :, :], ACT.Exp).then_inc(probs_ready, 1)

            def copy_PT(i):
                act.wait_ge(PT_ready, i + 1)
                act.activation(base_all[:, 0:2 * N], ps_PT, ACT.Copy).then_inc(PT_copied, 1)

            def split_oT(i):
                act.wait_ge(oT_ready, i + 1)
                act.activation(oT_hi[:, :, :].rearrange("p c n -> p (c n)"), ps_O, ACT.Copy).then_inc(oT_hi_ready, 1)

            def pair(i, score=True, qk=True):
                if score:
                    exp(i + 1)
                split_oT(i)
                if qk:
                    copy_KT(i + 2)
                if score:
                    copy_PT(i + 1)

            act.wait_ge(zeros_ready, 2)
            copy_KT(0)
            exp(0, first=True)
            copy_KT(1)
            copy_PT(0)
            pair(0)
            pair(1)
            with act.Fori(1, PAIRS // 2 - 1) as m:
                for k in range(2):
                    pair(m * 2 + k)
            pair(PAIRS - 2, qk=False)
            pair(PAIRS - 1, score=False, qk=False)

        @block.vector
        def _(dve):
            stt = dve.scalar_tensor_tensor

            def cube(n, src):
                dve.wait_ge(sq_ready, n + 1)
                stt(ps_cube, ps_cube, -3.0, src, ALU.add, ALU.mult).then_inc(cube_ready, 1)

            def tanh_split(n):
                dve.wait_ge(tanh_ready, n + 1)
                dve.tensor_tensor(tanh_lo[:, :], ps_tanh, tanh_hi[:, :].bitcast(F32), ALU.subtract).then_inc(tanh_lo_ready, 1)

            def b_of(n, s):
                dve.wait_ge(cube_ready, n + 1)
                stt(b_term[:, :], ps_cube, -A_STEP[s] / 3.0, base[s][:, :], ALU.mult, ALU.add).then_inc(b_ready, 1)

            def combine(dst, src, w, add):
                return stt(dst[:, :], src[:, :], w, add[:, :], ALU.mult, ALU.add)

            def next_q(n, s, dst, done):
                dve.wait_ge(b_ready, n + 1)
                dve.wait_ge(coupled, n + 1)
                stt(dst[:, :], ps_couple, A_STEP[s], b_term[:, :], ALU.mult, ALU.add).then_inc(done, 1)

            def norm_x(t):
                dve.wait_ge(rms_ready, t + 1)
                stt(xg[:, :], x1[:, :], rms[:, 0:1], gs_row[:, :], ALU.mult, ALU.mult).then_inc(xg_ready, 1)

            def split_xnT(t):
                dve.wait_ge(xnT_hi_ready, t + 1)
                flat = "p c n -> p (c n)"
                dve.tensor_tensor(xnT_lo[:, :, :].rearrange(flat), ps_xnT, xnT_hi[:, :, :].bitcast(F32).rearrange(flat),
                                  ALU.subtract).then_inc(xnT_lo_ready, 1)

            def sum_heads(t, part):
                j = 2 * t + part
                dve.wait_ge(head_sq_ready, j + 1)
                dve.tensor_reduce(head_sum[:, part * HEADS:(part + 1) * HEADS], head_sq[:, :].rearrange("p (h d) -> p h d", d=D),
                                  AX.X, ALU.add).then_inc(head_sum_ready, 1)

            RMS_OPS = 4 + 3 * 3

            def norm_heads(t, first=False):
                r0 = RMS_OPS * t
                dve.wait_ge(head_sum_ready, 2 * t + 2)
                dve.tensor_scalar(head_eps[:, :], head_sum[:, :], D * EPS, None, ALU.add).then_inc(head_rms_ready, 1)
                dve.tensor_scalar(head_half[:, :], head_sum[:, :], D * EPS, -0.5, ALU.add, ALU.mult).then_inc(head_rms_ready, 1)
                dve.wait_ge(head_rms_ready, r0 + 1)
                dve.tensor_scalar(head_tmp[:, :].bitcast(I32), head_eps[:, :].bitcast(I32), 1, None,
                                  ALU.logical_shift_right).then_inc(head_rms_ready, 1)
                dve.wait_ge(head_rms_ready, r0 + 3)
                dve.tensor_scalar(head_rms[:, :].bitcast(I32), head_tmp[:, :].bitcast(I32), -1.0, float(0x5F3759DF),
                                  ALU.mult, ALU.add).then_inc(head_rms_ready, 1)
                for j in range(3):
                    dve.wait_ge(head_rms_ready, r0 + 4 + 3 * j)
                    dve.tensor_tensor(head_tmp[:, :], head_rms[:, :], head_rms[:, :], ALU.mult).then_inc(head_rms_ready, 1)
                    dve.wait_ge(head_rms_ready, r0 + 5 + 3 * j)
                    dve.tensor_tensor(head_tmp[:, :], head_tmp[:, :], head_half[:, :], ALU.mult).then_inc(head_rms_ready, 1)
                    dve.wait_ge(head_rms_ready, r0 + 6 + 3 * j)
                    stt(head_rms[:, :], head_tmp[:, :], 1.5, head_rms[:, :], ALU.add, ALU.mult).then_inc(head_rms_ready, 1)
                dve.wait_ge(head_rms_ready, r0 + RMS_OPS)
                if not first:
                    dve.wait_ge(qk_stored, 16 * t)
                dve.tensor_tensor(qk_row[:, :].rearrange("p (h d) -> p h d", d=D),
                                  psum[:, 5:7, :].rearrange("p a (h d) -> p (a h) d", d=D),
                                  head_rms[:, :].unsqueeze(2).to_broadcast([P, 2 * HEADS, D]), ALU.mult).then_inc(qk_ready, 1)

            dve.wait_ge(cond_in, 16)
            dve.tensor_copy(q[0][:, :], q[1][:, :]).then_inc(q_ready, 1)
            dve.tensor_scalar(p_state[:, :], q[1][:, :], -P_SHIFT, None, ALU.add).then_inc(combos, 1)
            dve.wait_ge(rows_in, 48)
            dve.tensor_scalar(bias_row[:, :], bias_row[:, :], -P_SHIFT, None, ALU.add).then_inc(bias_ready, 1)
            for c in range(C):
                dve.wait_ge(coup_hi_ready, c + 1)
                dve.tensor_tensor(couple_lo[:, c, :], psum[:, c, :], couple_hi[:, c, :].bitcast(F32), ALU.subtract).then_inc(coup_split, 1)
            dve.wait_ge(emb_done, 2)
            dve.tensor_tensor(shift_row[:, :], psum[:, 6, :], emb_bias[:, N:2 * N], ALU.add).then_inc(emb_read, 1)
            dve.tensor_tensor(emb_bias[:, 0:N], psum[:, 5, :], emb_bias[:, 0:N], ALU.add).then_inc(emb_read, 1)
            dve.wait_ge(emb_read, 2)
            stt(gs_row[:, :], emb_bias[:, 0:N], 1.0, gs_row[:, :], ALU.add, ALU.mult).then_inc(emb_step, 1)
            dve.wait_ge(emb_step, 1)
            dve.tensor_scalar(gs_row[:, :], gs_row[:, :], float(np.sqrt(N)), None, ALU.mult).then_inc(emb_step, 1)
            dve.wait_ge(gcols_in, 16 * 2 * HG)
            dve.tensor_tensor(gqk_col[:, :], gq_col[:, :], gk_col[:, :], ALU.mult).then_inc(gqk_step, 1)
            dve.wait_ge(gqk_step, 1)
            dve.tensor_scalar(gqk_col[:, :], gqk_col[:, :], float(D) * float(D) ** -0.5, None, ALU.mult).then_inc(gqk_ready, 1)
            dve.wait_ge(emb_step, 2)

            def step(t, fill_two, fill_one, two_first=False):
                n = t * STAGES
                c0 = COMBOS * t + 1

                cube(n, q[0][:, :])
                if fill_two:
                    sum_heads(t - 2, 0)
                dve.wait_ge(combos, c0)
                combine(p_sum, q[0], P_NEXT[Q1] / P_NEXT[PP], p_state).then_inc(combos, 1)
                tanh_split(n)
                dve.wait_ge(base_ready, 4 * t + 1)
                b_of(n, 0)
                if fill_one:
                    norm_x(t - 1)
                next_q(n, 0, q[1], q_ready)

                cube(n + 1, q[1][:, :])
                if fill_two:
                    sum_heads(t - 2, 1)
                tanh_split(n + 1)
                dve.wait_ge(base_ready, 4 * t + 2)
                b_of(n + 1, 1)
                if fill_two:
                    norm_heads(t - 2, two_first)
                next_q(n + 1, 1, q[2], q_ready)

                cube(n + 2, q[2][:, :])
                dve.wait_ge(base_ready, 4 * t + 3)
                combine(base[2], q[1], BASE[2][Q2], base[2]).then_inc(combos, 1)
                dve.wait_ge(combos, c0 + 1)
                combine(p_sum, q[1], P_NEXT[Q2] / P_NEXT[PP], p_sum).then_inc(combos, 1)
                tanh_split(n + 2)
                dve.wait_ge(combos, c0 + 2)
                b_of(n + 2, 2)
                dve.wait_ge(base_ready, 4 * t + 4)
                combine(base[3], q[1], BASE[3][Q2], base[3]).then_inc(combos, 1)
                if fill_one:
                    split_xnT(t - 1)
                dve.wait_ge(combos, c0 + 4)
                combine(base[3], q[2], BASE[3][Q3], base[3]).then_inc(combos, 1)
                next_q(n + 2, 2, q[3], q_ready)

                dve.wait_ge(combos, c0 + 3)
                combine(p_sum, q[2], P_NEXT[Q3] / P_NEXT[PP], p_sum).then_inc(combos, 1)
                dve.wait_ge(q_ready, n + 4)
                dve.wait_ge(combos, c0 + 6)
                combine(p_sum, q[3], P_NEXT[Q4] / P_NEXT[PP], p_sum).then_inc(combos, 1)
                dve.wait_ge(combos, c0 + 7)
                dve.tensor_scalar(p_sum[:, :], p_sum[:, :], P_NEXT[PP], CLAMP - P_SHIFT, ALU.mult, ALU.min).then_inc(combos, 1)
                dve.wait_ge(combos, c0 + 8)
                dve.wait_ge(p_s_ready, 4 * t + 4)
                dve.tensor_scalar(p_state[:, :], p_sum[:, :], -CLAMP - P_SHIFT, None, ALU.max).then_inc(combos, 1)
                cube(n + 3, q[3][:, :])
                tanh_split(n + 3)
                dve.wait_ge(combos, c0 + 5)
                combine(base[3], q[3], BASE[3][Q4], base[3]).then_inc(combos, 1)
                dve.wait_ge(combos, c0 + 10)
                b_of(n + 3, 3)
                next_q(n + 3, 3, qraw, combos)
                dve.wait_ge(combos, c0 + 11)
                if fill_one:
                    dve.wait_ge(x1_ready, t)
                dve.tensor_scalar(q[0][:, :], qraw[:, :], CLAMP, -CLAMP, ALU.min, ALU.max).then_inc(q_ready, 1)

            step(0, False, False)
            for c in range(C):
                dve.wait_ge(wqkv_hi_ready, c + 1)
                o = dve.tensor_tensor(wqkv_lo[:, c, :], wqkv_nat[:, c, :], wqkv_hi[:, c, :].bitcast(F32), ALU.subtract)
            o.then_inc(wqkv_split, 1)
            step(1, False, True)
            dve.wait_ge(wout_hi_ready, 1)
            dve.tensor_tensor(wout_lo[:, :, :], wout_f32[:, :, :], wout_hi[:, :, :].bitcast(F32), ALU.subtract).then_inc(wout_split, 1)
            step(2, True, True, two_first=True)
            step(3, True, True)
            with dve.Fori(2, T // 2) as m:
                for k in range(2):
                    step(m * 2 + k, True, True)
            sum_heads(T - 2, 0)
            norm_x(T - 1)
            sum_heads(T - 2, 1)
            norm_heads(T - 2)
            split_xnT(T - 1)
            sum_heads(T - 1, 0)
            sum_heads(T - 1, 1)
            norm_heads(T - 1)

            def scale_QT(i):
                dve.wait_ge(QKT_ready, i + 1)
                dve.tensor_scalar(QT[:, :, :].rearrange("p g n -> p (g n)"), ps_QT, gqk_col[:, 0:1], None, ALU.mult).then_inc(QT_copied, 1)

            def shift(i):
                S = ps_S.rearrange("p (h k) -> p h k", k=T)
                dve.wait_ge(S_ready, i + 1)
                dve.tensor_reduce(neg_max[:, :], S, AX.X, ALU.max, negate=True).then_inc(max_ready, 1)
                dve.wait_ge(max_ready, i + 1)
                dve.tensor_tensor(shifted[:, :, :], S, neg_max[:, :].unsqueeze(2).to_broadcast([P, HEADS, T]),
                                  ALU.add).then_inc(shifted_ready, 1)

            def sum_probs(i):
                dve.wait_ge(probs_ready, i + 1)
                dve.tensor_reduce(row_sum[:, :], probs[:, :, :], AX.X, ALU.add).then_inc(sum_ready, 1)
                dve.wait_ge(sum_ready, i + 1)
                dve.reciprocal(row_rcp[:, :], row_sum[:, :]).then_inc(rcp_ready, 1)

            def norm_o(i, first=False):
                dve.wait_ge(rcp_ready, i + 1)
                dve.wait_ge(O_ready, i + 1)
                if not first:
                    dve.wait_ge(resid_ready, i)
                dve.tensor_tensor(o_row[:, :].rearrange("p (h d) -> p h d", d=D), ps_O.rearrange("p (h d) -> p h d", d=D),
                                  row_rcp[:, :].unsqueeze(2).to_broadcast([P, HEADS, D]), ALU.mult).then_inc(o_ready, 1)

            def split_oT(i):
                dve.wait_ge(oT_hi_ready, i + 1)
                flat = "p c n -> p (c n)"
                dve.tensor_tensor(oT_lo[:, :, :].rearrange(flat), ps_O, oT_hi[:, :, :].bitcast(F32).rearrange(flat),
                                  ALU.subtract).then_inc(oT_lo_ready, 1)

            def finish(i, k, m, fresh=False):
                dve.wait_ge(Y_ready, i + 1)
                dve.wait_ge(resid_ready, i + 1)
                if not fresh:
                    dve.wait_ge(y_stored[k], 16 * m)
                dve.tensor_tensor(y_row[k], ps_Y, resid[:, :], ALU.add).then_inc(y_ready, 1)

            def pair(i, k, m, score=True, qk=True, fresh=False, first=False):
                if score:
                    shift(i + 1)
                norm_o(i, first)
                if qk:
                    scale_QT(i + 2)
                split_oT(i)
                if score:
                    sum_probs(i + 1)
                finish(i, k, m, fresh)

            scale_QT(0)
            shift(0)
            scale_QT(1)
            sum_probs(0)
            pair(0, 0, 0, fresh=True, first=True)
            pair(1, 1, 0, fresh=True)
            with dve.Fori(1, PAIRS // 2 - 1) as m:
                for k in range(2):
                    pair(m * 2 + k, k, m)
            pair(PAIRS - 2, 0, PAIRS // 2 - 1, qk=False)
            pair(PAIRS - 1, 1, PAIRS // 2 - 1, score=False, qk=False)

        @block.gpsimd
        def _(pool):
            def add(dst, a, b):
                return pool.tensor_tensor(dst[:, :], a[:, :], b[:, :], ALU.add)

            def add_p(t, s, first=False):
                if s == 0:
                    pool.wait_ge(drive_s_ready, t + 1)
                    if not first:
                        pool.wait_ge(b_ready, 4 * t)
                pool.wait_ge(p_s_ready, 4 * t + s + 1)
                add(base[s], drive_s[(0, 0, 1, 2)[s]], p_s[s]).then_inc(pd_ready, 1)

            def add_q1(t, s):
                if s == 0:
                    pool.wait_ge(q_ready, 4 * t + 1)
                else:
                    pool.wait_ge(q1_s_ready, 3 * t + s)
                pool.wait_ge(pd_ready, 4 * t + s + 1)
                add(base[s], base[s], q[0] if s == 0 else q1_s[s - 1]).then_inc(base_ready, 1)

            def make_drive(t, k, m, first=False):
                pool.wait_ge(x_loaded[k], 16 * m + 16)
                if not first:
                    pool.wait_ge(drive_s_ready, t)
                add(drive, x_in[k], bias_row).then_inc(drive_ready, 1)

            def make_x1(t, k, first=False):
                pool.wait_ge(q_ready, 4 * t + 5)
                if not first:
                    pool.wait_ge(x1_stored, 16 * t)
                add(x1, x_in[k], q[0]).then_inc(x1_ready, 1)

            def rms_x(t, first=False):
                pool.wait_ge(sumsq_ready, t + 1)
                if first:
                    pool.wait_ge(half_ready, 2)
                pool.tensor_tensor(sumsq_eps[:, :], sumsq[:, :], eps_col[:, :], ALU.add).then_inc(sumsq_eps_ready, 1)
                pool.wait_ge(sumsq_eps_ready, t + 1)
                pool.tensor_tensor(rms[:, :], sumsq_eps[:, :], minus_half[:, :], ALU.pow).then_inc(rms_ready, 1)

            def shift_x(t, first=False):
                pool.wait_ge(xg_ready, t + 1)
                if not first:
                    pool.wait_ge(xnT_ready, t)
                add(xn, xg, shift_row).then_inc(xn_ready, 1)

            pool.memset(ident[:, :], 0.0).then_inc(ident_zero, 1)
            pool.wait_ge(ident_zero, 1)
            pool.affine_select(out=ident[:, :], in_=ident[:, :], compare_op=ALU.not_equal, fill=1.0,
                               base=0, pattern=[[-1, P]], channel_multiplier=1).then_inc(ident_ready, 1)
            pool.memset(minus_half[:, :], -0.5).then_inc(half_ready, 1)
            pool.memset(eps_col[:, :], N * EPS).then_inc(half_ready, 1)
            pool.wait_ge(bias_ready, 1)
            make_drive(0, 0, 0, first=True)
            add_p(0, 0, first=True)
            pool.memset(v_row[:, :, :], 0.0).then_inc(zeros_ready, 1)

            def step(t, k, m, last, fill_one, x_first=False):
                add_q1(t, 0)
                if fill_one:
                    make_x1(t - 1, 1 - k, x_first)
                add_p(t, 1)
                if fill_one:
                    rms_x(t - 1, x_first)
                add_q1(t, 1)
                if fill_one:
                    if x_first:
                        pool.wait_ge(emb_read, 2)
                    shift_x(t - 1, x_first)
                add_p(t, 2)
                add_q1(t, 2)
                if not last:
                    make_drive(t + 1, 1 - k, m + k)
                add_p(t, 3)
                add_q1(t, 3)
                if not last:
                    add_p(t + 1, 0)

            step(0, 0, 0, False, False)
            step(1, 1, 0, False, True, x_first=True)
            pool.wait_ge(wqkv_split, 1)
            pool.memset(KT_diag[:, :, :, :, :], 0.0).then_inc(zeros_ready, 1)
            with pool.Fori(1, T // 2 - 1) as m:
                for k in range(2):
                    step(m * 2 + k, k, m, False, True)
            step(T - 2, 0, T // 2 - 1, False, True)
            step(T - 1, 1, T // 2 - 1, True, True)
            make_x1(T - 1, 1)
            rms_x(T - 1)
            shift_x(T - 1)

            def residual(i, k, m, first=False):
                pool.wait_ge(o_ready, i + 1)
                pool.wait_ge(x1_loaded[k], 16 * m + 16)
                if not first:
                    pool.wait_ge(y_ready, i)
                add(resid, o_row, x1_in[k]).then_inc(resid_ready, 1)

            residual(0, 0, 0, first=True)
            residual(1, 1, 0)
            with pool.Fori(1, PAIRS // 2) as m:
                for k in range(2):
                    residual(m * 2 + k, k, m)


_INS = ["x", "cond_2048", "L0_cond_coupling", "L0_cond_bias", "L1_cond_W_emb", "L1_cond_b_emb", "L1_cond_g_norm",
        "L1_cond_W_qkv", "L1_cond_g_q", "L1_cond_g_k", "L1_cond_W_out"]


def kernel(**inputs):
    import numpy as _np
    import concourse.bacc as _bacc
    from concourse import mybir as _mybir
    from concourse.bass_utils import run_bass_kernel_spmd as _run

    nc = _bacc.Bacc("TRN2", target_bir_lowering=False, num_devices=1)
    arrays, args = {}, []
    for name in _INS:
        a = _np.ascontiguousarray(inputs[name])
        arrays[f"in_{name}"] = a
        args.append(nc.dram_tensor(f"in_{name}", a.shape, _mybir.dt.from_np(a.dtype), kind="ExternalInput").ap())
    shape = inputs["x"].shape
    args.append(nc.dram_tensor("out_0", shape, _mybir.dt.float32, kind="ExternalOutput").ap())
    fhn_attention_kernel(nc, *args)
    r = _run(nc, [arrays], core_ids=[0])
    return r.results[0]["out_0"]
```

```python
from contextlib import ExitStack

import numpy as np

import concourse.bass as bass
from concourse import mybir

F32 = mybir.dt.float32
F32R = mybir.dt.float32r
I32 = mybir.dt.int32
ALU = mybir.AluOpType
ACT = mybir.ActivationFunctionType
AX = mybir.AxisListType

P = 128
DT, EPSILON, ALPHA, BETA, CLAMP = 0.01, 0.08, 0.7, 0.8, 20.0
HEADS, EPS = 16, 1e-6
STAGES = 4
P_SHIFT = ALPHA / BETA


def rk4_weights():
    q1, q2, q3, q4, p, drive = np.eye(6)
    half = 0.5 * DT

    def dp(q, p_stage):
        return EPSILON * (q - BETA * p_stage)

    p2 = p + half * dp(q1, p)
    p3 = p + half * dp(q2, p2)
    p4 = p + DT * dp(q3, p3)
    p_next = p + DT / 6.0 * (dp(q1, p) + 2 * dp(q2, p2) + 2 * dp(q3, p3) + dp(q4, p4))
    base = [
        q1 + half * (drive - p),
        q1 + half * (drive - p2),
        q1 + DT * (drive - p3),
        (q2 + 2 * q3 + q4 - q1) / 3.0 + DT / 6.0 * (drive - p4),
    ]
    step = [half, half, DT, DT / 6.0]
    return step, [[float(v) for v in b] for b in base], [float(v) for v in p_next]


def fhn_attention_kernel(nc, x, cond, coupling, bias, w_emb, b_emb, g_norm, w_qkv, g_q, g_k, w_out, out):
    B, T, N = x.shape
    C = N // P
    D = N // HEADS
    HG = P // D
    G = HEADS // HG
    HP = HEADS // 2
    PAIRS = B * T // P
    assert B == P and 2 * T == P and C * P == N and G == C
    A_STEP, BASE, P_NEXT = rk4_weights()
    Q1, Q2, Q3, Q4, PP, DR = range(6)
    COMBOS = 9

    x1_scratch = nc.dram_tensor("x1_scratch", (B, T, N), F32, kind="Internal").ap()
    qk_scratch = nc.dram_tensor("qk_scratch", (B, T, 2 * N), F32, kind="Internal").ap()
    v_scratch = nc.dram_tensor("v_scratch", (B, 2, T, N), F32, kind="Internal").ap()

    with ExitStack() as ctx:
        def sb(name, shape, dt=F32):
            return ctx.enter_context(nc.sbuf_tensor(name, shape, dt))

        def sem(name):
            return ctx.enter_context(nc.semaphore(name))

        psum = ctx.enter_context(nc.psum_tensor("psum", [P, 8, 512], F32))
        ps_couple, ps_qT, ps_cube, ps_tanh, ps_xnT = (psum[:, n, :] for n in range(5))
        ps_qkv = [psum[:, 5 + n, :] for n in range(3)]
        ps_QT, ps_KT, ps_O, ps_Y = psum[:, 0, :], psum[:, 1, :], psum[:, 6, :], psum[:, 7, :]
        ps_S = psum[:, 2:4, :].rearrange("p a n -> p (a n)")
        ps_PT = psum[:, 4:6, :].rearrange("p a n -> p (a n)")

        ident = sb("ident", [P, P])
        bias_row = sb("bias_row", [P, N])
        gs_row = sb("gs_row", [P, N])
        shift_row = sb("shift_row", [P, N])
        emb_bias = sb("emb_bias", [P, 2 * N])
        gq_col = sb("gq_col", [P, 1])
        gk_col = sb("gk_col", [P, 1])
        gqk_col = sb("gqk_col", [P, 1])
        condT = sb("condT", [P, C, P])
        stage_w = sb("stage_w", [P, C, 3 * N])
        wout_f32 = sb("wout_f32", [P, C, N])
        couple_hi = sb("couple_hi", [P, C, N], F32R)
        couple_lo = sb("couple_lo", [P, C, N], F32R)
        wqkv_hi = sb("wqkv_hi", [P, C, 3 * N], F32R)
        wqkv_lo = sb("wqkv_lo", [P, C, 3 * N], F32R)
        wout_hi = sb("wout_hi", [P, C, N], F32R)
        wout_lo = sb("wout_lo", [P, C, N], F32R)

        q = [sb(f"q{s + 1}", [P, N]) for s in range(STAGES)]
        p_state = sb("p_state", [P, N])
        p_sum = sb("p_sum", [P, N])
        qraw = sb("qraw", [P, N])
        b_term = sb("b_term", [P, N])
        tanh_hi = sb("tanh_hi", [P, N], F32R)
        tanh_lo = sb("tanh_lo", [P, N], F32R)
        x_in = [sb(f"x_in{k}", [P, N]) for k in range(2)]
        drive = sb("drive", [P, N])
        drive_s = [sb(f"drive_s{n}", [P, N]) for n in range(3)]
        q1_s = [sb(f"q1_s{s}", [P, N]) for s in range(STAGES)]
        base_all = sb("base_all", [P, STAGES * N])
        base = [base_all[:, s * N:(s + 1) * N] for s in range(STAGES)]
        p_s3 = sb("p_s3", [P, N])
        p_s = [base[0], base[1], base[2], p_s3[:, :], p_sum[:, :]]
        x1 = sb("x1", [P, N])
        sq_dump = condT[:, :, :].rearrange("p c n -> p (c n)")
        sumsq = sb("sumsq", [P, 1])
        sumsq_eps = sb("sumsq_eps", [P, 1])
        minus_half = sb("minus_half", [P, 1])
        eps_col = sb("eps_col", [P, 1])
        rms = sb("rms", [P, 1])
        xg = sb("xg", [P, N])
        xn = sb("xn", [P, N])
        xnT_hi = sb("xnT_hi", [P, C, P], F32R)
        xnT_lo = sb("xnT_lo", [P, C, P], F32R)
        head_sq = sb("head_sq", [P, N])
        head_sum = sb("head_sum", [P, 2 * HEADS])
        head_eps = sb("head_eps", [P, 2 * HEADS])
        head_half = sb("head_half", [P, 2 * HEADS])
        head_rms = sb("head_rms", [P, 2 * HEADS])
        head_tmp = sb("head_tmp", [P, 2 * HEADS])
        qk_row = sb("qk_row", [P, 2 * N])
        v_row = sb("v_row", [P, 2, N])

        staged = stage_w[:, :, :].rearrange("p c n -> p (c n)")
        staged_out = wout_f32[:, :, :].rearrange("p c n -> p (c n)")
        qk_in = [staged[:, 2 * k * N:2 * (k + 1) * N] for k in range(2)]
        v_in = [staged[:, (4 + 2 * k) * N:(6 + 2 * k) * N].rearrange("p (b n) -> p b n", b=2) for k in range(2)]
        KT_diag = staged[:, 8 * N:12 * N].rearrange("p (g b h k) -> p g b h k", g=G, b=2, h=HG)
        PT = base_all[:, 0:2 * N].rearrange("p (h n) -> p h n", h=HP)
        shifted = base_all[:, 2 * N:4 * N].rearrange("p (h k) -> p h k", h=HEADS)
        probs = staged_out[:, 0:2 * N].rearrange("p (h k) -> p h k", h=HEADS)
        y_row = [staged_out[:, (2 + k) * N:(3 + k) * N] for k in range(2)]
        x1_in = [sb(f"x1_in{k}", [P, N]) for k in range(2)]
        QT = sb("QT", [P, G, P])
        neg_max = sb("neg_max", [P, HEADS])
        row_sum = sb("row_sum", [P, HEADS])
        row_rcp = sb("row_rcp", [P, HEADS])
        o_row, resid, oT_hi, oT_lo = xn, xg, xnT_hi, xnT_lo

        cond_in, couple_in, wqkv_in, wout_in, wemb_in, rows_in, gcols_in = (
            sem(n) for n in ("cond_in", "couple_in", "wqkv_in", "wout_in", "wemb_in", "rows_in", "gcols_in"))
        ident_zero, ident_ready, zeros_ready = sem("ident_zero"), sem("ident_ready"), sem("zeros_ready")
        coupT_ready, coup_hi_ready, coup_split = sem("coupT_ready"), sem("coup_hi_ready"), sem("coup_split")
        condT_done, condT_copied = sem("condT_done"), sem("condT_copied")
        emb_done, emb_read, emb_step = sem("emb_done"), sem("emb_read"), sem("emb_step")
        wqkv_hi_ready, wqkv_split = sem("wqkv_hi_ready"), sem("wqkv_split")
        wout_hi_ready, wout_split = sem("wout_hi_ready"), sem("wout_split")
        bias_ready, gqk_ready, gqk_step = sem("bias_ready"), sem("gqk_ready"), sem("gqk_step")
        q_ready, qT_ready, tanh_hi_ready, tanh_ready, tanh_lo_ready, coupled = (
            sem(n) for n in ("q_ready", "qT_ready", "tanh_hi_ready", "tanh_ready", "tanh_lo_ready", "coupled"))
        sq_ready, cube_ready, b_ready, combos = sem("sq_ready"), sem("cube_ready"), sem("b_ready"), sem("combos")
        drive_ready, drive_s_ready, p_s_ready, q1_s_ready = (
            sem(n) for n in ("drive_ready", "drive_s_ready", "p_s_ready", "q1_s_ready"))
        pd_ready, base_ready, p_sum_ready, qk_copied = sem("pd_ready"), sem("base_ready"), sem("p_sum_ready"), sem("qk_copied")
        x_loaded = [sem(f"x_loaded{k}") for k in range(2)]
        x1_ready, x1_stored, sumsq_ready, rms_ready, xg_ready, xn_ready, xnT_ready = (
            sem(n) for n in ("x1_ready", "x1_stored", "sumsq_ready", "rms_ready", "xg_ready", "xn_ready", "xnT_ready"))
        xnT_hi_ready, xnT_lo_ready, qkv_done = sem("xnT_hi_ready"), sem("xnT_lo_ready"), sem("qkv_done")
        head_sq_ready, head_sum_ready, head_rms_ready, qk_ready, v_ready = (
            sem(n) for n in ("head_sq_ready", "head_sum_ready", "head_rms_ready", "qk_ready", "v_ready"))
        half_ready, sumsq_eps_ready = sem("half_ready"), sem("sumsq_eps_ready")
        qk_stored, v_stored = sem("qk_stored"), sem("v_stored")
        qk_loaded, v_loaded, x1_loaded, y_stored = (
            [sem(f"{n}{k}") for k in range(2)] for n in ("qk_loaded", "v_loaded", "x1_loaded", "y_stored"))
        QKT_ready, QT_copied, KT_copied, S_ready, max_ready, shifted_ready, probs_ready = (
            sem(n) for n in ("QKT_ready", "QT_copied", "KT_copied", "S_ready", "max_ready", "shifted_ready", "probs_ready"))
        sum_ready, rcp_ready, PT_ready, PT_copied, O_ready, o_ready, oT_ready = (
            sem(n) for n in ("sum_ready", "rcp_ready", "PT_ready", "PT_copied", "O_ready", "o_ready", "oT_ready"))
        oT_hi_ready, oT_lo_ready, Y_ready, resid_ready, y_ready = (
            sem(n) for n in ("oT_hi_ready", "oT_lo_ready", "Y_ready", "resid_ready", "y_ready"))

        coupling_nat = stage_w[:, :, 0:N]
        wemb_nat = stage_w[:, :, N:3 * N]
        wqkv_nat = stage_w[:, :, :]

        def rows(t):
            return bass.ds(t, 1)

        block = ctx.enter_context(nc.Block())

        @block.sync
        def _(sp):
            sp.dma_start(coupling_nat, coupling.rearrange("(c n) m -> n c m", c=C)).then_inc(couple_in, 16)
            sp.dma_start(q[1][:, :], cond).then_inc(cond_in, 16)
            sp.dma_start(x_in[0][:, :], x[:, 0, :]).then_inc(x_loaded[0], 16)
            sp.dma_start(x_in[1][:, :], x[:, 1, :]).then_inc(x_loaded[1], 16)
            sp.dma_start(bias_row[:, :], bias.partition_broadcast(P)).then_inc(rows_in, 16)
            sp.dma_start(gs_row[:, :], g_norm.partition_broadcast(P)).then_inc(rows_in, 16)
            sp.dma_start(emb_bias[:, :], b_emb.partition_broadcast(P)).then_inc(rows_in, 16)
            sp.dma_start(wemb_nat, w_emb.rearrange("(c p) n -> p c n", c=C)).then_inc(wemb_in, 16)
            sp.dma_start(wout_f32[:, :, :], w_out.rearrange("(c p) n -> p c n", c=C)).then_inc(wout_in, 16)
            for h in range(HG):
                sp.dma_start(gq_col[h * D:(h + 1) * D, :], g_q.unsqueeze(1)).then_inc(gcols_in, 16)
                sp.dma_start(gk_col[h * D:(h + 1) * D, :], g_k.unsqueeze(1)).then_inc(gcols_in, 16)
            sp.wait_ge(coupT_ready, C)
            sp.wait_ge(emb_done, 2)
            sp.dma_start(wqkv_nat, w_qkv.rearrange("(c p) n -> p c n", c=C)).then_inc(wqkv_in, 16)

            def load_x(t, k):
                sp.wait_ge(x1_ready, t - 1)
                sp.dma_start(x_in[k][:, :], x[:, rows(t), :].rearrange("b o n -> b (o n)")).then_inc(x_loaded[k], 16)

            def store_x1(t):
                sp.wait_ge(x1_ready, t + 1)
                sp.dma_start(x1_scratch[:, rows(t), :].rearrange("b o n -> b (o n)"), x1[:, :]).then_inc(x1_stored, 16)

            def store_qk(t):
                sp.wait_ge(qk_ready, t + 1)
                sp.dma_start(qk_scratch[:, rows(t), :].rearrange("b o n -> b (o n)"), qk_row[:, :]).then_inc(qk_stored, 16)

            def store_v(t):
                sp.wait_ge(v_ready, t + 1)
                sp.dma_start(v_scratch[:, :, rows(t), :].rearrange("b e o n -> b e (o n)"), v_row[:, :, :]).then_inc(v_stored, 16)

            def step(t, k, store_old, ahead=True):
                if store_old:
                    store_qk(t - 3)
                if ahead:
                    load_x(t + 1, 1 - k)
                store_x1(t - 1)
                store_v(t - 2)

            load_x(2, 0)
            store_x1(0)
            step(2, 0, False)
            step(3, 1, True)
            with sp.Fori(2, T // 2 - 1) as m:
                for k in range(2):
                    step(m * 2 + k, k, True)
            step(T - 2, 0, True)
            step(T - 1, 1, True, ahead=False)
            store_qk(T - 3)
            store_x1(T - 1)
            store_v(T - 2)
            store_qk(T - 2)
            store_v(T - 1)
            store_qk(T - 1)

            sp.wait_ge(qk_stored, 16 * T)
            sp.wait_ge(v_stored, 16 * T)
            sp.wait_ge(x1_stored, 16 * T)
            x1_tok = x1_scratch.rearrange("(i b) t n -> i (b t) n", b=2)
            qk_tok = qk_scratch.rearrange("(i b) t n -> i (b t) n", b=2)
            v_tok = v_scratch.rearrange("(i b) e t n -> i (e t) b n", b=2)
            y_tok = out.rearrange("(i b) t n -> i (b t) n", b=2)

            def tile_of(a, i):
                return a[bass.ds(i, 1)]

            def load_qk(i, k):
                sp.dma_start(qk_in[k], tile_of(qk_tok, i).rearrange("o p n -> (o p) n")).then_inc(qk_loaded[k], 16)

            def load_vx(i, k):
                sp.dma_start(v_in[k], tile_of(v_tok, i).rearrange("o p b n -> (o p) b n")).then_inc(v_loaded[k], 16)
                sp.dma_start(x1_in[k][:, :], tile_of(x1_tok, i).rearrange("o p n -> (o p) n")).then_inc(x1_loaded[k], 16)

            def store_y(i, k):
                sp.wait_ge(y_ready, i + 1)
                sp.dma_start(tile_of(y_tok, i).rearrange("o p n -> (o p) n"), y_row[k]).then_inc(y_stored[k], 16)

            load_qk(0, 0)
            load_qk(1, 1)
            load_vx(0, 0)
            sp.wait_ge(QKT_ready, 1)
            load_qk(2, 0)

            def steady(i, k, qk, store):
                if qk:
                    sp.wait_ge(QKT_ready, i + 2)
                    load_qk(i + 3, 1 - k)
                if store:
                    sp.wait_ge(O_ready, i)
                    sp.wait_ge(resid_ready, i)
                load_vx(i + 1, 1 - k)
                if store:
                    store_y(i - 1, 1 - k)

            steady(0, 0, True, False)
            steady(1, 1, True, True)
            with sp.Fori(1, PAIRS // 2 - 2) as m:
                for k in range(2):
                    steady(m * 2 + k, k, True, True)
            steady(PAIRS - 4, 0, True, True)
            steady(PAIRS - 3, 1, False, True)
            steady(PAIRS - 2, 0, False, True)
            store_y(PAIRS - 2, 0)
            store_y(PAIRS - 1, 1)
            for k in range(2):
                sp.wait_ge(y_stored[k], 16 * (PAIRS // 2))

        @block.tensor
        def _(pe):
            def couple(n):
                for c in range(C):
                    if c == 0:
                        pe.wait_ge(tanh_hi_ready, n + 1)
                    pe.matmul(ps_couple, tanh_hi[:, c * P:(c + 1) * P], couple_hi[:, c, :], start=(c == 0), stop=False)
                for c in range(C):
                    pe.matmul(ps_couple, tanh_hi[:, c * P:(c + 1) * P], couple_lo[:, c, :], start=False, stop=False)
                for c in range(C):
                    if c == 0:
                        pe.wait_ge(tanh_lo_ready, n + 1)
                    mm = pe.matmul(ps_couple, tanh_lo[:, c * P:(c + 1) * P], couple_hi[:, c, :], start=False, stop=(c == C - 1))
                mm.then_inc(coupled, 1)

            def transpose_q(n, src):
                pe.wait_ge(q_ready, n + 1)
                for c in range(C):
                    mm = pe.transpose(ps_qT[:, c * P:(c + 1) * P], src[:, c * P:(c + 1) * P], ident[:, :])
                mm.then_inc(qT_ready, 1)

            PRODUCTS = [(a, w, c) for a, w in ((xnT_hi, wqkv_hi), (xnT_hi, wqkv_lo), (xnT_lo, wqkv_hi)) for c in range(C)]

            def project(t, lo, hi):
                for j in range(lo, hi):
                    part, r = divmod(j, len(PRODUCTS))
                    a, w, c = PRODUCTS[r]
                    if j == 0:
                        pe.wait_ge(xnT_lo_ready, t + 1)
                        if not (isinstance(t, int) and t == 0):
                            pe.wait_ge(qk_copied, t)
                    if r == 0 and part == 2 and not (isinstance(t, int) and t == 0):
                        pe.wait_ge(v_ready, t)
                    mm = pe.matmul(ps_qkv[part], a[:, c, :], w[:, c, part * N:(part + 1) * N],
                                   start=(r == 0), stop=(r == len(PRODUCTS) - 1))
                    if r == len(PRODUCTS) - 1:
                        mm.then_inc(qkv_done, 1)

            def transpose_xn(t):
                pe.wait_ge(xn_ready, t + 1)
                for c in range(C):
                    mm = pe.transpose(ps_xnT[:, c * P:(c + 1) * P], xn[:, c * P:(c + 1) * P], ident[:, :])
                mm.then_inc(xnT_ready, 1)

            pe.wait_ge(ident_ready, 1)
            pe.wait_ge(couple_in, 16)
            for c in range(C):
                for g in range(C):
                    mm = pe.transpose(psum[:, c, g * P:(g + 1) * P], coupling_nat[:, g, c * P:(c + 1) * P], ident[:, :])
                mm.then_inc(coupT_ready, 1)
            pe.wait_ge(cond_in, 16)
            for c in range(C):
                mm = pe.transpose(psum[:, 4, c * P:(c + 1) * P], q[1][:, c * P:(c + 1) * P], ident[:, :])
            mm.then_inc(condT_done, 1)
            pe.wait_ge(wemb_in, 16)
            pe.wait_ge(condT_copied, 1)
            for half in range(2):
                for c in range(C):
                    mm = pe.matmul(psum[:, 5 + half, :], condT[:, c, :], wemb_nat[:, c, half * N:(half + 1) * N],
                                   start=(c == 0), stop=(c == C - 1))
                mm.then_inc(emb_done, 1)
            pe.wait_ge(coup_split, C)
            transpose_q(0, q[0])

            def step(t, stages_ahead, fill_two, fill_one):
                n = t * STAGES
                for s in range(STAGES):
                    couple(n + s)
                    old = fill_two and s < 2
                    new = fill_one and s >= 2
                    lo = 18 + 9 * s if old else 9 * (s - 2)
                    tt = t - 2 if old else t - 1
                    if old or new:
                        project(tt, lo, lo + 4)
                    if s < STAGES - 1 or stages_ahead:
                        transpose_q(n + s + 1, q[(s + 1) % STAGES])
                    if old or new:
                        project(tt, lo + 4, lo + 9)
                    if s == 1 and fill_one:
                        transpose_xn(t - 1)

            pe.wait_ge(emb_read, 2)
            step(0, True, False, False)
            pe.wait_ge(wqkv_split, 1)
            step(1, True, False, True)
            with pe.Fori(1, T // 2 - 1) as m:
                for k in range(2):
                    step(m * 2 + k, True, True, True)
            step(T - 2, True, True, True)
            step(T - 1, False, True, True)
            project(T - 2, 18, 36)
            transpose_xn(T - 1)
            project(T - 1, 0, 36)

            def transpose_qk(i, k, m):
                pe.wait_ge(qk_loaded[k], 16 * m + 16)
                for g in range(G):
                    pe.transpose(ps_QT[:, g * P:(g + 1) * P], qk_in[k][:, g * P:(g + 1) * P], ident[:, :])
                for g in range(G):
                    mm = pe.transpose(ps_KT[:, g * P:(g + 1) * P], qk_in[k][:, N + g * P:N + (g + 1) * P], ident[:, :])
                mm.then_inc(QKT_ready, 1)

            def scores(i):
                pe.wait_ge(QT_copied, i + 1)
                pe.wait_ge(KT_copied, i + 1)
                for g in range(G):
                    for b in range(2):
                        mm = pe.matmul(ps_S[b * T:(b + 1) * T, g * HG * T:(g + 1) * HG * T],
                                       QT[:, g, b * T:(b + 1) * T],
                                       KT_diag[:, g, b, :, :].rearrange("p h k -> p (h k)"), start=True, stop=True)
                mm.then_inc(S_ready, 1)

            def transpose_probs(i):
                pe.wait_ge(probs_ready, i + 1)
                for hp in range(HP):
                    mm = pe.transpose(ps_PT[:, hp * P:(hp + 1) * P],
                                      probs[:, 2 * hp:2 * hp + 2, :].rearrange("p h k -> p (h k)"), ident[:, :])
                mm.then_inc(PT_ready, 1)

            def attend(i, k, m):
                pe.wait_ge(PT_copied, i + 1)
                pe.wait_ge(v_loaded[k], 16 * m + 16)
                for hp in range(HP):
                    for b in range(2):
                        mm = pe.matmul(ps_O[b * T:(b + 1) * T, hp * 2 * D:(hp + 1) * 2 * D],
                                       PT[:, hp, b * T:(b + 1) * T], v_in[k][:, b, hp * 2 * D:(hp + 1) * 2 * D],
                                       start=True, stop=True)
                mm.then_inc(O_ready, 1)

            def transpose_o(i):
                pe.wait_ge(o_ready, i + 1)
                for c in range(C):
                    mm = pe.transpose(ps_O[:, c * P:(c + 1) * P], o_row[:, c * P:(c + 1) * P], ident[:, :])
                mm.then_inc(oT_ready, 1)

            def project_out(i, first):
                if not first:
                    pe.wait_ge(y_ready, i)
                for j, (a, w) in enumerate(((oT_hi, wout_hi), (oT_hi, wout_lo), (oT_lo, wout_hi))):
                    if j == 0:
                        pe.wait_ge(oT_hi_ready, i + 1)
                    if j == 2:
                        pe.wait_ge(oT_lo_ready, i + 1)
                    for c in range(C):
                        mm = pe.matmul(ps_Y, a[:, c, :], w[:, c, :], start=(j == 0 and c == 0), stop=(j == 2 and c == C - 1))
                mm.then_inc(Y_ready, 1)

            def pair(i, k, m, first=False, score=True, qk=True):
                if score:
                    scores(i + 1)
                attend(i, k, m)
                if qk:
                    transpose_qk(i + 2, k, m + 1)
                transpose_o(i)
                if score:
                    transpose_probs(i + 1)
                project_out(i, first)

            pe.wait_ge(qk_ready, T)
            pe.wait_ge(v_ready, T)
            transpose_qk(0, 0, 0)
            scores(0)
            transpose_qk(1, 1, 0)
            transpose_probs(0)
            pe.wait_ge(wout_split, 1)
            pair(0, 0, 0, first=True)
            pair(1, 1, 0)
            with pe.Fori(1, PAIRS // 2 - 1) as m:
                for k in range(2):
                    pair(m * 2 + k, k, m)
            pair(PAIRS - 2, 0, PAIRS // 2 - 1, qk=False)
            pair(PAIRS - 1, 1, PAIRS // 2 - 1, score=False, qk=False)

        @block.scalar
        def _(act):
            def square_q(n, src):
                act.wait_ge(q_ready, n + 1)
                act.activation(ps_cube, src, ACT.Square).then_inc(sq_ready, 1)

            def tanh(n):
                act.wait_ge(qT_ready, n + 1)
                act.activation(tanh_hi[:, :], ps_qT, ACT.Tanh).then_inc(tanh_hi_ready, 1)
                act.activation(ps_tanh, ps_qT, ACT.Tanh).then_inc(tanh_ready, 1)

            def scale_drive(t, first=False):
                act.wait_ge(drive_ready, t + 1)
                if not first:
                    act.wait_ge(pd_ready, 4 * t)
                for n, f in enumerate((BASE[0][DR], BASE[2][DR], BASE[3][DR])):
                    o = act.activation(drive_s[n][:, :], drive[:, :], ACT.Copy, scale=f)
                o.then_inc(drive_s_ready, 1)

            def scale_p(t, first=False):
                act.wait_ge(combos, COMBOS * t - 2 if not first else 1)
                if not first:
                    act.wait_ge(pd_ready, 4 * t)
                for dst, w in zip(p_s, [BASE[s][PP] for s in range(STAGES)] + [P_NEXT[PP]]):
                    act.activation(dst, p_state[:, :], ACT.Copy, scale=w).then_inc(p_s_ready, 1)

            def scale_q1(t, first=False):
                if not first:
                    act.wait_ge(base_ready, 4 * t)
                for dst, w in zip(q1_s, (BASE[1][Q1], BASE[2][Q1], P_NEXT[Q1], BASE[3][Q1])):
                    act.activation(dst[:, :], q[0][:, :], ACT.Copy, scale=w).then_inc(q1_s_ready, 1)

            def square_x1(t):
                act.wait_ge(x1_ready, t + 1)
                act.activation(sq_dump, x1[:, :], ACT.Square, accum_out=sumsq[:, :]).then_inc(sumsq_ready, 1)

            def square_heads(t, part, first=False):
                act.wait_ge(qkv_done, 3 * t + part + 1)
                if not first:
                    act.wait_ge(head_sum_ready, 2 * t + part)
                act.activation(head_sq[:, :], ps_qkv[part], ACT.Square).then_inc(head_sq_ready, 1)

            def copy_qk(t, first=False):
                act.wait_ge(qkv_done, 3 * t + 2)
                if not first:
                    act.wait_ge(qk_stored, 16 * t)
                act.activation(qk_row[:, :], psum[:, 5:7, :].rearrange("p a n -> p (a n)"), ACT.Copy).then_inc(qk_copied, 1)

            def split_xnT(t):
                act.wait_ge(xnT_ready, t + 1)
                act.activation(xnT_hi[:, :, :].rearrange("p c n -> p (c n)"), ps_xnT, ACT.Copy).then_inc(xnT_hi_ready, 1)

            def copy_v(t, first=False):
                act.wait_ge(qkv_done, 3 * t + 3)
                if not first:
                    act.wait_ge(v_stored, 16 * t)
                else:
                    act.wait_ge(zeros_ready, 1)
                v = ps_qkv[2].rearrange("p (h e d) -> p h e d", e=2, d=D)
                for e in range(2):
                    o = act.activation(v_row[:, e, :].rearrange("p (h e d) -> p h e d", e=2, d=D)[:, :, e, :],
                                       v[:, :, e, :], ACT.Copy)
                o.then_inc(v_ready, 1)

            for c in range(C):
                act.wait_ge(coupT_ready, c + 1)
                act.activation(couple_hi[:, c, :], psum[:, c, :], ACT.Copy).then_inc(coup_hi_ready, 1)
            act.wait_ge(condT_done, 1)
            act.activation(condT[:, :, :].rearrange("p c n -> p (c n)"), psum[:, 4, :], ACT.Copy).then_inc(condT_copied, 1)
            act.wait_ge(coup_split, C)
            scale_p(0, first=True)
            scale_drive(0, first=True)

            def step(t, last, fill_two, fill_one, two_first=False, first=False):
                n = t * STAGES
                square_q(n, q[0][:, :])
                tanh(n)
                if fill_one:
                    square_x1(t - 1)
                if fill_two:
                    square_heads(t - 2, 0, two_first)
                scale_q1(t, first)
                square_q(n + 1, q[1][:, :])
                tanh(n + 1)
                if fill_two:
                    square_heads(t - 2, 1)
                    copy_qk(t - 2, two_first)
                square_q(n + 2, q[2][:, :])
                tanh(n + 2)
                if fill_one:
                    split_xnT(t - 1)
                if not last:
                    scale_drive(t + 1)
                if fill_two:
                    copy_v(t - 2, two_first)
                square_q(n + 3, q[3][:, :])
                tanh(n + 3)
                if not last:
                    scale_p(t + 1)

            step(0, False, False, False, first=True)
            act.wait_ge(wqkv_in, 16)
            for c in range(C):
                for part in range(3):
                    o = act.activation(wqkv_hi[:, c, part * N:(part + 1) * N], wqkv_nat[:, c, part * N:(part + 1) * N], ACT.Copy)
                o.then_inc(wqkv_hi_ready, 1)
            step(1, False, False, True)
            act.wait_ge(wout_in, 16)
            for c in range(C):
                o = act.activation(wout_hi[:, c, :], wout_f32[:, c, :], ACT.Copy)
            o.then_inc(wout_hi_ready, 1)
            step(2, False, True, True, two_first=True)
            step(3, False, True, True)
            with act.Fori(2, T // 2 - 1) as m:
                for k in range(2):
                    step(m * 2 + k, False, True, True)
            step(T - 2, False, True, True)
            step(T - 1, True, True, True)
            square_heads(T - 2, 0)
            square_x1(T - 1)
            square_heads(T - 2, 1)
            copy_qk(T - 2)
            copy_v(T - 2)
            split_xnT(T - 1)
            square_heads(T - 1, 0)
            square_heads(T - 1, 1)
            copy_qk(T - 1)
            copy_v(T - 1)

            def copy_KT(i):
                act.wait_ge(QKT_ready, i + 1)
                for h in range(HG):
                    r = slice(h * D, (h + 1) * D)
                    o = act.activation(KT_diag[r, :, :, h, :], ps_KT[r, :].rearrange("p (g b k) -> p g b k", g=G, b=2), ACT.Copy)
                o.then_inc(KT_copied, 1)

            def exp(i, first=False):
                act.wait_ge(shifted_ready, i + 1)
                if not first:
                    act.wait_ge(PT_ready, i)
                    act.wait_ge(sum_ready, i)
                act.activation(probs[:, :, :], shifted[:, :, :], ACT.Exp).then_inc(probs_ready, 1)

            def copy_PT(i):
                act.wait_ge(PT_ready, i + 1)
                act.activation(base_all[:, 0:2 * N], ps_PT, ACT.Copy).then_inc(PT_copied, 1)

            def split_oT(i):
                act.wait_ge(oT_ready, i + 1)
                act.activation(oT_hi[:, :, :].rearrange("p c n -> p (c n)"), ps_O, ACT.Copy).then_inc(oT_hi_ready, 1)

            def pair(i, score=True, qk=True):
                if score:
                    exp(i + 1)
                split_oT(i)
                if qk:
                    copy_KT(i + 2)
                if score:
                    copy_PT(i + 1)

            act.wait_ge(zeros_ready, 2)
            copy_KT(0)
            exp(0, first=True)
            copy_KT(1)
            copy_PT(0)
            pair(0)
            pair(1)
            with act.Fori(1, PAIRS // 2 - 1) as m:
                for k in range(2):
                    pair(m * 2 + k)
            pair(PAIRS - 2, qk=False)
            pair(PAIRS - 1, score=False, qk=False)

        @block.vector
        def _(dve):
            stt = dve.scalar_tensor_tensor

            def cube(n, src):
                dve.wait_ge(sq_ready, n + 1)
                stt(ps_cube, ps_cube, -3.0, src, ALU.add, ALU.mult).then_inc(cube_ready, 1)

            def tanh_split(n):
                dve.wait_ge(tanh_ready, n + 1)
                dve.tensor_tensor(tanh_lo[:, :], ps_tanh, tanh_hi[:, :].bitcast(F32), ALU.subtract).then_inc(tanh_lo_ready, 1)

            def b_of(n, s):
                dve.wait_ge(cube_ready, n + 1)
                stt(b_term[:, :], ps_cube, -A_STEP[s] / 3.0, base[s][:, :], ALU.mult, ALU.add).then_inc(b_ready, 1)

            def combine(dst, src, w, add):
                return stt(dst[:, :], src[:, :], w, add[:, :], ALU.mult, ALU.add)

            def next_q(n, s, dst, done):
                dve.wait_ge(b_ready, n + 1)
                dve.wait_ge(coupled, n + 1)
                stt(dst[:, :], ps_couple, A_STEP[s], b_term[:, :], ALU.mult, ALU.add).then_inc(done, 1)

            def norm_x(t):
                dve.wait_ge(rms_ready, t + 1)
                stt(xg[:, :], x1[:, :], rms[:, 0:1], gs_row[:, :], ALU.mult, ALU.mult).then_inc(xg_ready, 1)

            def split_xnT(t):
                dve.wait_ge(xnT_hi_ready, t + 1)
                flat = "p c n -> p (c n)"
                dve.tensor_tensor(xnT_lo[:, :, :].rearrange(flat), ps_xnT, xnT_hi[:, :, :].bitcast(F32).rearrange(flat),
                                  ALU.subtract).then_inc(xnT_lo_ready, 1)

            def sum_heads(t, part):
                j = 2 * t + part
                dve.wait_ge(head_sq_ready, j + 1)
                dve.tensor_reduce(head_sum[:, part * HEADS:(part + 1) * HEADS], head_sq[:, :].rearrange("p (h d) -> p h d", d=D),
                                  AX.X, ALU.add).then_inc(head_sum_ready, 1)

            NEWTON_STEPS = 3
            RMS_OPS = 4 + 3 * NEWTON_STEPS

            def head_root(t, lo=0, hi=RMS_OPS):
                r0 = RMS_OPS * t
                for j in range(lo, hi):
                    if j == 0:
                        dve.wait_ge(head_sum_ready, 2 * t + 2)
                        o = dve.tensor_scalar(head_eps[:, :], head_sum[:, :], D * EPS, None, ALU.add)
                    elif j == 1:
                        o = dve.tensor_scalar(head_half[:, :], head_sum[:, :], D * EPS, -0.5, ALU.add, ALU.mult)
                    elif j == 2:
                        dve.wait_ge(head_rms_ready, r0 + 1)
                        o = dve.tensor_scalar(head_tmp[:, :].bitcast(I32), head_eps[:, :].bitcast(I32), 1, None,
                                              ALU.logical_shift_right)
                    elif j == 3:
                        dve.wait_ge(head_rms_ready, r0 + 3)
                        o = dve.tensor_scalar(head_rms[:, :].bitcast(I32), head_tmp[:, :].bitcast(I32), -1.0,
                                              float(0x5F3759DF), ALU.mult, ALU.add)
                    else:
                        dve.wait_ge(head_rms_ready, r0 + j)
                        if j % 3 == 1:
                            o = dve.tensor_tensor(head_tmp[:, :], head_rms[:, :], head_rms[:, :], ALU.mult)
                        elif j % 3 == 2:
                            o = dve.tensor_tensor(head_tmp[:, :], head_tmp[:, :], head_half[:, :], ALU.mult)
                        else:
                            o = stt(head_rms[:, :], head_tmp[:, :], 1.5, head_rms[:, :], ALU.add, ALU.mult)
                    o.then_inc(head_rms_ready, 1)

            def norm_heads(t):
                dve.wait_ge(head_rms_ready, RMS_OPS * (t + 1))
                dve.wait_ge(qk_copied, t + 1)
                row = qk_row[:, :].rearrange("p (h d) -> p h d", d=D)
                dve.tensor_tensor(row, row, head_rms[:, :].unsqueeze(2).to_broadcast([P, 2 * HEADS, D]),
                                  ALU.mult).then_inc(qk_ready, 1)

            dve.wait_ge(cond_in, 16)
            dve.tensor_copy(q[0][:, :], q[1][:, :]).then_inc(q_ready, 1)
            dve.tensor_scalar(p_state[:, :], q[1][:, :], -P_SHIFT, None, ALU.add).then_inc(combos, 1)
            dve.wait_ge(rows_in, 48)
            dve.tensor_scalar(bias_row[:, :], bias_row[:, :], -P_SHIFT, None, ALU.add).then_inc(bias_ready, 1)
            for c in range(C):
                dve.wait_ge(coup_hi_ready, c + 1)
                dve.tensor_tensor(couple_lo[:, c, :], psum[:, c, :], couple_hi[:, c, :].bitcast(F32), ALU.subtract).then_inc(coup_split, 1)
            dve.wait_ge(emb_done, 2)
            dve.tensor_tensor(shift_row[:, :], psum[:, 6, :], emb_bias[:, N:2 * N], ALU.add).then_inc(emb_read, 1)
            dve.tensor_tensor(emb_bias[:, 0:N], psum[:, 5, :], emb_bias[:, 0:N], ALU.add).then_inc(emb_read, 1)
            dve.wait_ge(emb_read, 2)
            stt(gs_row[:, :], emb_bias[:, 0:N], 1.0, gs_row[:, :], ALU.add, ALU.mult).then_inc(emb_step, 1)
            dve.wait_ge(emb_step, 1)
            dve.tensor_scalar(gs_row[:, :], gs_row[:, :], float(np.sqrt(N)), None, ALU.mult).then_inc(emb_step, 1)
            dve.wait_ge(gcols_in, 16 * 2 * HG)
            dve.tensor_tensor(gqk_col[:, :], gq_col[:, :], gk_col[:, :], ALU.mult).then_inc(gqk_step, 1)
            dve.wait_ge(gqk_step, 1)
            dve.tensor_scalar(gqk_col[:, :], gqk_col[:, :], float(D) * float(D) ** -0.5, None, ALU.mult).then_inc(gqk_ready, 1)
            dve.wait_ge(emb_step, 2)

            def step(t, fill_three, fill_two, fill_one):
                n = t * STAGES
                c0 = COMBOS * t + 1

                if fill_three:
                    norm_heads(t - 3)
                cube(n, q[0][:, :])
                tanh_split(n)
                dve.wait_ge(base_ready, 4 * t + 1)
                b_of(n, 0)
                if fill_two:
                    sum_heads(t - 2, 0)
                next_q(n, 0, q[1], q_ready)

                if fill_one:
                    norm_x(t - 1)
                cube(n + 1, q[1][:, :])
                tanh_split(n + 1)
                dve.wait_ge(base_ready, 4 * t + 2)
                b_of(n + 1, 1)
                dve.wait_ge(base_ready, 4 * t + 3)
                combine(base[2], q[1], BASE[2][Q2], base[2]).then_inc(combos, 1)
                if fill_two:
                    sum_heads(t - 2, 1)
                    head_root(t - 2, 0, 2)
                next_q(n + 1, 1, q[2], q_ready)

                dve.wait_ge(p_sum_ready, t + 1)
                combine(p_sum, q[1], P_NEXT[Q2], p_sum).then_inc(combos, 1)
                if fill_two:
                    head_root(t - 2, 2, 3)
                cube(n + 2, q[2][:, :])
                if fill_two:
                    head_root(t - 2, 3, 4)
                dve.wait_ge(combos, c0 + 2)
                combine(p_sum, q[2], P_NEXT[Q3], p_sum).then_inc(combos, 1)
                if fill_two:
                    head_root(t - 2, 4, 5)
                tanh_split(n + 2)
                if fill_two:
                    head_root(t - 2, 5, 6)
                dve.wait_ge(combos, c0 + 1)
                b_of(n + 2, 2)
                if fill_two:
                    head_root(t - 2, 6, 7)
                if fill_one:
                    split_xnT(t - 1)
                if fill_two:
                    head_root(t - 2, 7, 8)
                dve.wait_ge(base_ready, 4 * t + 4)
                combine(base[3], q[1], BASE[3][Q2], base[3]).then_inc(combos, 1)
                if fill_two:
                    head_root(t - 2, 8, 9)
                next_q(n + 2, 2, q[3], q_ready)

                if fill_two:
                    head_root(t - 2, 9, 10)
                dve.wait_ge(q_ready, n + 4)
                dve.wait_ge(combos, c0 + 3)
                combine(p_sum, q[3], P_NEXT[Q4], p_sum).then_inc(combos, 1)
                if fill_two:
                    head_root(t - 2, 10, 11)
                dve.wait_ge(combos, c0 + 5)
                dve.wait_ge(p_s_ready, 5 * t + 5)
                dve.tensor_scalar(p_state[:, :], p_sum[:, :], CLAMP - P_SHIFT, -CLAMP - P_SHIFT, ALU.min, ALU.max).then_inc(combos, 1)
                cube(n + 3, q[3][:, :])
                dve.wait_ge(combos, c0 + 4)
                combine(base[3], q[2], BASE[3][Q3], base[3]).then_inc(combos, 1)
                if fill_two:
                    head_root(t - 2, 11, 12)
                tanh_split(n + 3)
                dve.wait_ge(combos, c0 + 7)
                combine(base[3], q[3], BASE[3][Q4], base[3]).then_inc(combos, 1)
                if fill_two:
                    head_root(t - 2, 12, 13)
                dve.wait_ge(combos, c0 + 8)
                b_of(n + 3, 3)
                next_q(n + 3, 3, qraw, combos)
                dve.wait_ge(combos, c0 + 9)
                if fill_one:
                    dve.wait_ge(x1_ready, t)
                dve.tensor_scalar(q[0][:, :], qraw[:, :], CLAMP, -CLAMP, ALU.min, ALU.max).then_inc(q_ready, 1)

            step(0, False, False, False)
            for c in range(C):
                dve.wait_ge(wqkv_hi_ready, c + 1)
                o = dve.tensor_tensor(wqkv_lo[:, c, :], wqkv_nat[:, c, :], wqkv_hi[:, c, :].bitcast(F32), ALU.subtract)
            o.then_inc(wqkv_split, 1)
            step(1, False, False, True)
            dve.wait_ge(wout_hi_ready, 1)
            dve.tensor_tensor(wout_lo[:, :, :], wout_f32[:, :, :], wout_hi[:, :, :].bitcast(F32), ALU.subtract).then_inc(wout_split, 1)
            step(2, False, True, True)
            step(3, True, True, True)
            with dve.Fori(2, T // 2) as m:
                for k in range(2):
                    step(m * 2 + k, True, True, True)
            norm_heads(T - 3)
            sum_heads(T - 2, 0)
            norm_x(T - 1)
            sum_heads(T - 2, 1)
            head_root(T - 2)
            norm_heads(T - 2)
            split_xnT(T - 1)
            sum_heads(T - 1, 0)
            sum_heads(T - 1, 1)
            head_root(T - 1)
            norm_heads(T - 1)

            def scale_QT(i):
                dve.wait_ge(QKT_ready, i + 1)
                dve.tensor_scalar(QT[:, :, :].rearrange("p g n -> p (g n)"), ps_QT, gqk_col[:, 0:1], None, ALU.mult).then_inc(QT_copied, 1)

            def shift(i):
                S = ps_S.rearrange("p (h k) -> p h k", k=T)
                dve.wait_ge(S_ready, i + 1)
                dve.tensor_reduce(neg_max[:, :], S, AX.X, ALU.max, negate=True).then_inc(max_ready, 1)
                dve.wait_ge(max_ready, i + 1)
                dve.tensor_tensor(shifted[:, :, :], S, neg_max[:, :].unsqueeze(2).to_broadcast([P, HEADS, T]),
                                  ALU.add).then_inc(shifted_ready, 1)

            def sum_probs(i):
                dve.wait_ge(probs_ready, i + 1)
                dve.tensor_reduce(row_sum[:, :], probs[:, :, :], AX.X, ALU.add).then_inc(sum_ready, 1)
                dve.wait_ge(sum_ready, i + 1)
                dve.reciprocal(row_rcp[:, :], row_sum[:, :]).then_inc(rcp_ready, 1)

            def norm_o(i, first=False):
                dve.wait_ge(rcp_ready, i + 1)
                dve.wait_ge(O_ready, i + 1)
                if not first:
                    dve.wait_ge(resid_ready, i)
                dve.tensor_tensor(o_row[:, :].rearrange("p (h d) -> p h d", d=D), ps_O.rearrange("p (h d) -> p h d", d=D),
                                  row_rcp[:, :].unsqueeze(2).to_broadcast([P, HEADS, D]), ALU.mult).then_inc(o_ready, 1)

            def split_oT(i):
                dve.wait_ge(oT_hi_ready, i + 1)
                flat = "p c n -> p (c n)"
                dve.tensor_tensor(oT_lo[:, :, :].rearrange(flat), ps_O, oT_hi[:, :, :].bitcast(F32).rearrange(flat),
                                  ALU.subtract).then_inc(oT_lo_ready, 1)

            def finish(i, k, m, fresh=False):
                dve.wait_ge(Y_ready, i + 1)
                dve.wait_ge(resid_ready, i + 1)
                if not fresh:
                    dve.wait_ge(y_stored[k], 16 * m)
                dve.tensor_tensor(y_row[k], ps_Y, resid[:, :], ALU.add).then_inc(y_ready, 1)

            def pair(i, k, m, score=True, qk=True, fresh=False, first=False):
                if score:
                    shift(i + 1)
                norm_o(i, first)
                if qk:
                    scale_QT(i + 2)
                split_oT(i)
                if score:
                    sum_probs(i + 1)
                finish(i, k, m, fresh)

            scale_QT(0)
            shift(0)
            scale_QT(1)
            sum_probs(0)
            pair(0, 0, 0, fresh=True, first=True)
            pair(1, 1, 0, fresh=True)
            with dve.Fori(1, PAIRS // 2 - 1) as m:
                for k in range(2):
                    pair(m * 2 + k, k, m)
            pair(PAIRS - 2, 0, PAIRS // 2 - 1, qk=False)
            pair(PAIRS - 1, 1, PAIRS // 2 - 1, score=False, qk=False)

        @block.gpsimd
        def _(pool):
            def add(dst, a, b):
                return pool.tensor_tensor(dst[:, :], a[:, :], b[:, :], ALU.add)

            def add_p(t, s, first=False):
                if s == 0:
                    pool.wait_ge(drive_s_ready, t + 1)
                if s == 3 and not first:
                    pool.wait_ge(b_ready, 4 * t)
                pool.wait_ge(p_s_ready, 5 * t + s + 1)
                pool.tensor_tensor(base[s], drive_s[(0, 0, 1, 2)[s]][:, :], p_s[s], ALU.add).then_inc(pd_ready, 1)

            def add_q1(t, s):
                if s == 0:
                    pool.wait_ge(q_ready, 4 * t + 1)
                    src = q[0]
                else:
                    pool.wait_ge(q1_s_ready, 4 * t + (0, 1, 2, 4)[s])
                    src = q1_s[(0, 0, 1, 3)[s]]
                pool.wait_ge(pd_ready, 4 * t + s + 1)
                add(base[s], base[s], src).then_inc(base_ready, 1)

            def start_p_sum(t):
                pool.wait_ge(p_s_ready, 5 * t + 5)
                pool.wait_ge(q1_s_ready, 4 * t + 3)
                add(p_sum, p_sum, q1_s[2]).then_inc(p_sum_ready, 1)

            def make_drive(t, k, m, first=False):
                pool.wait_ge(x_loaded[k], 16 * m + 16)
                if not first:
                    pool.wait_ge(drive_s_ready, t)
                add(drive, x_in[k], bias_row).then_inc(drive_ready, 1)

            def make_x1(t, k, first=False):
                pool.wait_ge(q_ready, 4 * t + 5)
                if not first:
                    pool.wait_ge(x1_stored, 16 * t)
                add(x1, x_in[k], q[0]).then_inc(x1_ready, 1)

            def rms_x(t, first=False):
                pool.wait_ge(sumsq_ready, t + 1)
                if first:
                    pool.wait_ge(half_ready, 2)
                pool.tensor_tensor(sumsq_eps[:, :], sumsq[:, :], eps_col[:, :], ALU.add).then_inc(sumsq_eps_ready, 1)
                pool.wait_ge(sumsq_eps_ready, t + 1)
                pool.tensor_tensor(rms[:, :], sumsq_eps[:, :], minus_half[:, :], ALU.pow).then_inc(rms_ready, 1)

            def shift_x(t, first=False):
                pool.wait_ge(xg_ready, t + 1)
                if not first:
                    pool.wait_ge(xnT_ready, t)
                add(xn, xg, shift_row).then_inc(xn_ready, 1)

            pool.memset(ident[:, :], 0.0).then_inc(ident_zero, 1)
            pool.wait_ge(ident_zero, 1)
            pool.affine_select(out=ident[:, :], in_=ident[:, :], compare_op=ALU.not_equal, fill=1.0,
                               base=0, pattern=[[-1, P]], channel_multiplier=1).then_inc(ident_ready, 1)
            pool.memset(minus_half[:, :], -0.5).then_inc(half_ready, 1)
            pool.memset(eps_col[:, :], N * EPS).then_inc(half_ready, 1)
            pool.wait_ge(bias_ready, 1)
            make_drive(0, 0, 0, first=True)
            add_p(0, 0)
            add_p(0, 1)
            pool.memset(v_row[:, :, :], 0.0).then_inc(zeros_ready, 1)

            def step(t, k, m, last, fill_one, x_first=False):
                add_q1(t, 0)
                if fill_one:
                    make_x1(t - 1, 1 - k, x_first)
                add_q1(t, 1)
                if fill_one:
                    rms_x(t - 1, x_first)
                add_p(t, 2)
                add_q1(t, 2)
                if fill_one:
                    if x_first:
                        pool.wait_ge(emb_read, 2)
                    shift_x(t - 1, x_first)
                start_p_sum(t)
                if not last:
                    make_drive(t + 1, 1 - k, m + k)
                add_p(t, 3, first=not fill_one)
                add_q1(t, 3)
                if not last:
                    add_p(t + 1, 0)
                    add_p(t + 1, 1)

            step(0, 0, 0, False, False)
            step(1, 1, 0, False, True, x_first=True)
            pool.wait_ge(wqkv_split, 1)
            pool.memset(KT_diag[:, :, :, :, :], 0.0).then_inc(zeros_ready, 1)
            with pool.Fori(1, T // 2 - 1) as m:
                for k in range(2):
                    step(m * 2 + k, k, m, False, True)
            step(T - 2, 0, T // 2 - 1, False, True)
            step(T - 1, 1, T // 2 - 1, True, True)
            make_x1(T - 1, 1)
            rms_x(T - 1)
            shift_x(T - 1)

            def residual(i, k, m, first=False):
                pool.wait_ge(o_ready, i + 1)
                pool.wait_ge(x1_loaded[k], 16 * m + 16)
                if not first:
                    pool.wait_ge(y_ready, i)
                add(resid, o_row, x1_in[k]).then_inc(resid_ready, 1)

            residual(0, 0, 0, first=True)
            residual(1, 1, 0)
            with pool.Fori(1, PAIRS // 2) as m:
                for k in range(2):
                    residual(m * 2 + k, k, m)


_INS = ["x", "cond_2048", "L0_cond_coupling", "L0_cond_bias", "L1_cond_W_emb", "L1_cond_b_emb", "L1_cond_g_norm",
        "L1_cond_W_qkv", "L1_cond_g_q", "L1_cond_g_k", "L1_cond_W_out"]


def kernel(**inputs):
    import numpy as _np
    import concourse.bacc as _bacc
    from concourse import mybir as _mybir
    from concourse.bass_utils import run_bass_kernel_spmd as _run

    nc = _bacc.Bacc("TRN2", target_bir_lowering=False, num_devices=1)
    arrays, args = {}, []
    for name in _INS:
        a = _np.ascontiguousarray(inputs[name])
        arrays[f"in_{name}"] = a
        args.append(nc.dram_tensor(f"in_{name}", a.shape, _mybir.dt.from_np(a.dtype), kind="ExternalInput").ap())
    shape = inputs["x"].shape
    args.append(nc.dram_tensor("out_0", shape, _mybir.dt.float32, kind="ExternalOutput").ap())
    fhn_attention_kernel(nc, *args)
    r = _run(nc, [arrays], core_ids=[0])
    return r.results[0]["out_0"]
```

```python
from contextlib import ExitStack

import numpy as np

import concourse.bass as bass
from concourse import mybir

F32 = mybir.dt.float32
F32R = mybir.dt.float32r
I32 = mybir.dt.int32
ALU = mybir.AluOpType
ACT = mybir.ActivationFunctionType
AX = mybir.AxisListType

P = 128
DT, EPSILON, ALPHA, BETA, CLAMP = 0.01, 0.08, 0.7, 0.8, 20.0
HEADS, EPS = 16, 1e-6
STAGES = 4
P_SHIFT = ALPHA / BETA


def rk4_weights():
    q1, q2, q3, q4, p, drive = np.eye(6)
    half = 0.5 * DT

    def dp(q, p_stage):
        return EPSILON * (q - BETA * p_stage)

    p2 = p + half * dp(q1, p)
    p3 = p + half * dp(q2, p2)
    p4 = p + DT * dp(q3, p3)
    p_next = p + DT / 6.0 * (dp(q1, p) + 2 * dp(q2, p2) + 2 * dp(q3, p3) + dp(q4, p4))
    base = [
        q1 + half * (drive - p),
        q1 + half * (drive - p2),
        q1 + DT * (drive - p3),
        (q2 + 2 * q3 + q4 - q1) / 3.0 + DT / 6.0 * (drive - p4),
    ]
    step = [half, half, DT, DT / 6.0]
    return step, [[float(v) for v in b] for b in base], [float(v) for v in p_next]


def fhn_attention_kernel(nc, x, cond, coupling, bias, w_emb, b_emb, g_norm, w_qkv, g_q, g_k, w_out, out):
    B, T, N = x.shape
    C = N // P
    D = N // HEADS
    HG = P // D
    G = HEADS // HG
    HP = HEADS // 2
    PAIRS = B * T // P
    assert B == P and 2 * T == P and C * P == N and G == C and (PAIRS - 4) % 6 == 0
    A_STEP, BASE, P_NEXT = rk4_weights()
    Q1, Q2, Q3, Q4, PP, DR = range(6)
    NEWTON_STEPS = 3
    ROOT_OPS = 4 + 3 * NEWTON_STEPS
    UNROLL = 6
    COMBOS = 11

    x1_scratch = nc.dram_tensor("x1_scratch", (B, T, N), F32, kind="Internal").ap()
    qk_scratch = nc.dram_tensor("qk_scratch", (B, T, 2 * N), F32, kind="Internal").ap()
    v_scratch = nc.dram_tensor("v_scratch", (B, 2, T, N), F32, kind="Internal").ap()

    with ExitStack() as ctx:
        def sb(name, shape, dt=F32):
            return ctx.enter_context(nc.sbuf_tensor(name, shape, dt))

        def sem(name):
            return ctx.enter_context(nc.semaphore(name))

        psum = ctx.enter_context(nc.psum_tensor("psum", [P, 8, 512], F32))
        ps_couple, ps_qT, ps_cube, ps_tanh, ps_xnT = (psum[:, n, :] for n in range(5))
        ps_qkv = [psum[:, 5 + n, :] for n in range(3)]
        ps_QT, ps_KT, ps_O, ps_Y = psum[:, 0, :], psum[:, 1, :], psum[:, 6, :], psum[:, 7, :]
        ps_S = psum[:, 2:4, :].rearrange("p a n -> p (a n)")
        ps_PT = psum[:, 4:6, :].rearrange("p a n -> p (a n)")

        ident = sb("ident", [P, P])
        bias_row = sb("bias_row", [P, N])
        gs_row = sb("gs_row", [P, N])
        shift_row = sb("shift_row", [P, N])
        emb_bias = sb("emb_bias", [P, 2 * N])
        gq_col = sb("gq_col", [P, 1])
        gk_col = sb("gk_col", [P, 1])
        gqk_col = sb("gqk_col", [P, 1])
        condT = sb("condT", [P, C, P])
        stage_w = sb("stage_w", [P, C, 3 * N])
        wout_f32 = sb("wout_f32", [P, C, N])
        couple_hi = sb("couple_hi", [P, C, N], F32R)
        couple_lo = sb("couple_lo", [P, C, N], F32R)
        wqkv_hi = sb("wqkv_hi", [P, C, 3 * N], F32R)
        wqkv_lo = sb("wqkv_lo", [P, C, 3 * N], F32R)
        wout_hi = sb("wout_hi", [P, C, N], F32R)
        wout_lo = sb("wout_lo", [P, C, N], F32R)

        q = [sb(f"q{s + 1}", [P, N]) for s in range(STAGES)]
        p_state = sb("p_state", [P, N])
        p_sum = sb("p_sum", [P, N])
        qraw = sb("qraw", [P, N])
        b_term = sb("b_term", [P, N])
        tanh_hi = sb("tanh_hi", [P, N], F32R)
        tanh_lo = sb("tanh_lo", [P, N], F32R)
        x_in = [sb(f"x_in{k}", [P, N]) for k in range(2)]
        drive = sb("drive", [P, N])
        drive_s = [sb(f"drive_s{n}", [P, N]) for n in range(3)]
        q1_s = [sb(f"q1_s{s}", [P, N]) for s in range(1, STAGES)]
        base_all = sb("base_all", [P, STAGES * N])
        base = [base_all[:, s * N:(s + 1) * N] for s in range(STAGES)]
        p_s3 = sb("p_s3", [P, N])
        p_s = [base[0], base[1], base[2], p_s3[:, :]]
        x1 = sb("x1", [P, N])
        sq_dump = condT[:, :, :].rearrange("p c n -> p (c n)")
        sumsq = sb("sumsq", [P, 1])
        sumsq_eps = sb("sumsq_eps", [P, 1])
        minus_half = sb("minus_half", [P, 1])
        eps_col = sb("eps_col", [P, 1])
        rms = sb("rms", [P, 1])
        xg = sb("xg", [P, N])
        xn = sb("xn", [P, N])
        xnT_hi = sb("xnT_hi", [P, C, P], F32R)
        xnT_lo = sb("xnT_lo", [P, C, P], F32R)
        head_sum = sb("head_sum", [P, 2 * HEADS])
        head_eps = sb("head_eps", [P, 2 * HEADS])
        head_half = sb("head_half", [P, 2 * HEADS])
        head_rms = sb("head_rms", [P, 2 * HEADS])
        head_tmp = sb("head_tmp", [P, 2 * HEADS])
        qk_row = sb("qk_row", [P, 2 * N])
        v_row = sb("v_row", [P, 2, N])

        staged = stage_w[:, :, :].rearrange("p c n -> p (c n)")
        staged_out = wout_f32[:, :, :].rearrange("p c n -> p (c n)")
        qk_in = [staged[:, 2 * k * N:2 * (k + 1) * N] for k in range(2)]
        v_in = [staged[:, (4 + 2 * k) * N:(6 + 2 * k) * N].rearrange("p (b n) -> p b n", b=2) for k in range(2)]
        qk_sq = v_row[:, :, :].rearrange("p e n -> p (e n)")
        qk_norm = qk_row
        KT_diag = staged[:, 8 * N:12 * N].rearrange("p (g b h k) -> p g b h k", g=G, b=2, h=HG)
        PT = base_all[:, 0:2 * N].rearrange("p (h n) -> p h n", h=HP)
        shifted = base_all[:, 2 * N:4 * N].rearrange("p (h k) -> p h k", h=HEADS)
        probs = staged_out[:, 0:2 * N].rearrange("p (h k) -> p h k", h=HEADS)
        y_row = [staged_out[:, (2 + k) * N:(3 + k) * N] for k in range(2)]
        x1_in = [sb(f"x1_in{k}", [P, N]) for k in range(2)]
        QT = sb("QT", [P, G, P])
        neg_max = sb("neg_max", [P, HEADS])
        row_sum = sb("row_sum", [P, HEADS])
        row_rcp = sb("row_rcp", [P, HEADS])
        resid = q[0:2]
        o_row, y_copy, oT_hi, oT_lo = xn, xg, xnT_hi, xnT_lo

        cond_in, couple_in, wqkv_in, wout_in, wemb_in, rows_in, gcols_in = (
            sem(n) for n in ("cond_in", "couple_in", "wqkv_in", "wout_in", "wemb_in", "rows_in", "gcols_in"))
        ident_zero, ident_ready, zeros_ready = sem("ident_zero"), sem("ident_ready"), sem("zeros_ready")
        coupT_ready, coup_hi_ready, coup_split = sem("coupT_ready"), sem("coup_hi_ready"), sem("coup_split")
        condT_done, condT_copied = sem("condT_done"), sem("condT_copied")
        emb_done, emb_read, emb_step = sem("emb_done"), sem("emb_read"), sem("emb_step")
        wqkv_hi_ready = sem("wqkv_hi_ready")
        wqkv_split = [sem(f"wqkv_split{part}") for part in range(3)]
        wout_hi_ready, wout_split = sem("wout_hi_ready"), sem("wout_split")
        bias_ready, gqk_ready, gqk_step = sem("bias_ready"), sem("gqk_ready"), sem("gqk_step")
        q_ready, qT_ready, tanh_hi_ready, tanh_ready, tanh_lo_ready, coupled = (
            sem(n) for n in ("q_ready", "qT_ready", "tanh_hi_ready", "tanh_ready", "tanh_lo_ready", "coupled"))
        sq_ready, cube_ready, b_ready, combos = sem("sq_ready"), sem("cube_ready"), sem("b_ready"), sem("combos")
        drive_ready, drive_s_ready, p_s_ready, q1_s_ready = (
            sem(n) for n in ("drive_ready", "drive_s_ready", "p_s_ready", "q1_s_ready"))
        pd_ready, base_ready, qk_copied = sem("pd_ready"), sem("base_ready"), sem("qk_copied")
        x_loaded = [sem(f"x_loaded{k}") for k in range(2)]
        x1_ready, x1_stored, sumsq_ready, rms_ready, xg_ready, xn_ready, xnT_ready = (
            sem(n) for n in ("x1_ready", "x1_stored", "sumsq_ready", "rms_ready", "xg_ready", "xn_ready", "xnT_ready"))
        xnT_hi_ready, xnT_lo_ready, qkv_done = sem("xnT_hi_ready"), sem("xnT_lo_ready"), sem("qkv_done")
        half_ready, sumsq_eps_ready = sem("half_ready"), sem("sumsq_eps_ready")
        v_ready, qk_stored, v_stored = sem("v_ready"), sem("qk_stored"), sem("v_stored")
        qk_loaded, v_loaded, x1_loaded, y_stored = (
            [sem(f"{n}{k}") for k in range(2)] for n in ("qk_loaded", "v_loaded", "x1_loaded", "y_stored"))
        QKT_ready, QT_copied, KT_copied, S_ready, max_ready, shifted_ready, probs_ready = (
            sem(n) for n in ("QKT_ready", "QT_copied", "KT_copied", "S_ready", "max_ready", "shifted_ready", "probs_ready"))
        qk_sq_ready, qk_sum_ready, qk_root, qkn_ready = (
            sem(n) for n in ("qk_sq_ready", "qk_sum_ready", "qk_root", "qkn_ready"))
        sum_ready, rcp_ready, PT_ready, PT_copied, O_ready, o_ready, oT_ready = (
            sem(n) for n in ("sum_ready", "rcp_ready", "PT_ready", "PT_copied", "O_ready", "o_ready", "oT_ready"))
        oT_hi_ready, oT_lo_ready, Y_ready, Y_copied, resid_ready, y_ready = (
            sem(n) for n in ("oT_hi_ready", "oT_lo_ready", "Y_ready", "Y_copied", "resid_ready", "y_ready"))

        coupling_nat = stage_w[:, :, 0:N]
        wemb_nat = [wout_f32[:, :, :], qk_row[:, :].rearrange("p (c n) -> p c n", n=N), v_row[:, :, :]]
        wqkv_nat = stage_w[:, :, :]

        def rows(t):
            return bass.ds(t, 1)

        block = ctx.enter_context(nc.Block())

        @block.sync
        def _(sp):
            sp.dma_start(coupling_nat, coupling.rearrange("(c n) m -> n c m", c=C)).then_inc(couple_in, 16)
            sp.dma_start(q[1][:, :], cond).then_inc(cond_in, 16)
            sp.dma_start(x_in[0][:, :], x[:, 0, :]).then_inc(x_loaded[0], 16)
            sp.dma_start(x_in[1][:, :], x[:, 1, :]).then_inc(x_loaded[1], 16)
            sp.dma_start(bias_row[:, :], bias.partition_broadcast(P)).then_inc(rows_in, 16)
            sp.dma_start(gs_row[:, :], g_norm.partition_broadcast(P)).then_inc(rows_in, 16)
            sp.dma_start(emb_bias[:, :], b_emb.partition_broadcast(P)).then_inc(rows_in, 16)
            wemb_rows = w_emb.rearrange("(c p) n -> p c n", c=C)
            sp.dma_start(wemb_nat[0], wemb_rows[:, :, 0:N]).then_inc(wemb_in, 16)
            for k in range(2):
                sp.dma_start(wemb_nat[1 + k], wemb_rows[:, 2 * k:2 * k + 2, N:2 * N]).then_inc(wemb_in, 16)
            for h in range(HG):
                sp.dma_start(gq_col[h * D:(h + 1) * D, :], g_q.unsqueeze(1)).then_inc(gcols_in, 16)
                sp.dma_start(gk_col[h * D:(h + 1) * D, :], g_k.unsqueeze(1)).then_inc(gcols_in, 16)
            sp.wait_ge(coupT_ready, C)
            sp.dma_start(wqkv_nat, w_qkv.rearrange("(c p) n -> p c n", c=C)).then_inc(wqkv_in, 16)
            sp.wait_ge(emb_done, 1)
            sp.dma_start(wout_f32[:, :, :], w_out.rearrange("(c p) n -> p c n", c=C)).then_inc(wout_in, 16)

            def load_x(t, k):
                sp.wait_ge(x1_ready, t - 1)
                sp.dma_start(x_in[k][:, :], x[:, rows(t), :].rearrange("b o n -> b (o n)")).then_inc(x_loaded[k], 16)

            def store_x1(t):
                sp.wait_ge(x1_ready, t + 1)
                sp.dma_start(x1_scratch[:, rows(t), :].rearrange("b o n -> b (o n)"), x1[:, :]).then_inc(x1_stored, 16)

            def store_qk(t):
                sp.wait_ge(qk_copied, t + 1)
                sp.dma_start(qk_scratch[:, rows(t), :].rearrange("b o n -> b (o n)"), qk_row[:, :]).then_inc(qk_stored, 16)

            def store_v(t):
                sp.wait_ge(v_ready, t + 1)
                sp.dma_start(v_scratch[:, :, rows(t), :].rearrange("b e o n -> b e (o n)"), v_row[:, :, :]).then_inc(v_stored, 16)

            def step(t, k, ahead=True):
                if ahead:
                    load_x(t + 1, 1 - k)
                store_x1(t - 1)
                store_qk(t - 2)
                store_v(t - 2)

            load_x(2, 0)
            store_x1(0)
            with sp.Fori(1, T // 2 - 1) as m:
                for k in range(2):
                    step(m * 2 + k, k)
            step(T - 2, 0)
            step(T - 1, 1, ahead=False)
            store_x1(T - 1)
            for t in (T - 2, T - 1):
                store_qk(t)
                store_v(t)

            x1_tok = x1_scratch.rearrange("(i b) t n -> i (b t) n", b=2)
            qk_tok = qk_scratch.rearrange("(i b) t n -> i (b t) n", b=2)
            v_tok = v_scratch.rearrange("(i b) e t n -> i (e t) b n", b=2)
            y_tok = out.rearrange("(i b) t n -> i (b t) n", b=2)

            def tile_of(a, i):
                return a[bass.ds(i, 1)]

            def load_qk(i, k):
                sp.dma_start(qk_in[k], tile_of(qk_tok, i).rearrange("o p n -> (o p) n")).then_inc(qk_loaded[k], 16)

            def load_vx(i, k):
                sp.dma_start(v_in[k], tile_of(v_tok, i).rearrange("o p b n -> (o p) b n")).then_inc(v_loaded[k], 16)
                sp.dma_start(x1_in[k][:, :], tile_of(x1_tok, i).rearrange("o p n -> (o p) n")).then_inc(x1_loaded[k], 16)

            def store_y(i, k):
                sp.wait_ge(y_ready, i + 1)
                sp.dma_start(tile_of(y_tok, i).rearrange("o p n -> (o p) n"), y_row[k]).then_inc(y_stored[k], 16)

            def refill_qk(i, k):
                sp.wait_ge(qkn_ready, i - 1)
                load_qk(i, k)

            sp.wait_ge(qk_stored, 16 * T)
            load_qk(0, 0)
            load_qk(1, 1)
            sp.wait_ge(v_stored, 16 * T)
            sp.wait_ge(x1_stored, 16 * T)
            load_vx(0, 0)
            refill_qk(2, 0)
            refill_qk(3, 1)

            def steady(i, k, qk=True, first=False, store=True):
                if qk:
                    refill_qk(i + 4, k)
                if not first:
                    sp.wait_ge(O_ready, i)
                    sp.wait_ge(resid_ready, i)
                load_vx(i + 1, 1 - k)
                if store:
                    store_y(i - 2, k)

            steady(0, 0, first=True, store=False)
            steady(1, 1, store=False)
            with sp.Fori(1, PAIRS // 2 - 2) as m:
                for k in range(2):
                    steady(m * 2 + k, k)
            for i in range(PAIRS - 4, PAIRS - 1):
                steady(i, i % 2, qk=False)
            for i in range(PAIRS - 3, PAIRS):
                store_y(i, i % 2)
            for k in range(2):
                sp.wait_ge(y_stored[k], 16 * (PAIRS // 2))

        @block.tensor
        def _(pe):
            def couple(n):
                for c in range(C):
                    if c == 0:
                        pe.wait_ge(tanh_hi_ready, n + 1)
                    pe.matmul(ps_couple, tanh_hi[:, c * P:(c + 1) * P], couple_hi[:, c, :], start=(c == 0), stop=False)
                for c in range(C):
                    pe.matmul(ps_couple, tanh_hi[:, c * P:(c + 1) * P], couple_lo[:, c, :], start=False, stop=False)
                for c in range(C):
                    if c == 0:
                        pe.wait_ge(tanh_lo_ready, n + 1)
                    mm = pe.matmul(ps_couple, tanh_lo[:, c * P:(c + 1) * P], couple_hi[:, c, :], start=False, stop=(c == C - 1))
                mm.then_inc(coupled, 1)

            def transpose_q(src, ready, count):
                pe.wait_ge(ready, count)
                for c in range(C):
                    mm = pe.transpose(ps_qT[:, c * P:(c + 1) * P], src[:, c * P:(c + 1) * P], ident[:, :])
                mm.then_inc(qT_ready, 1)

            PRODUCTS = [(a, w, c) for a, w in ((xnT_hi, wqkv_hi), (xnT_hi, wqkv_lo), (xnT_lo, wqkv_hi)) for c in range(C)]

            def project(t, lo, hi):
                for j in range(lo, hi):
                    part, r = divmod(j, len(PRODUCTS))
                    a, w, c = PRODUCTS[r]
                    if isinstance(t, int) and t == 0 and r == 0:
                        pe.wait_ge(wqkv_split[part], 1)
                        if part < 2:
                            pe.wait_ge(emb_read, 2)
                    if j == 0:
                        pe.wait_ge(xnT_lo_ready, t + 1)
                        if not (isinstance(t, int) and t == 0):
                            pe.wait_ge(qk_copied, t)
                    if r == 0 and part == 2 and not (isinstance(t, int) and t == 0):
                        pe.wait_ge(v_ready, t)
                    mm = pe.matmul(ps_qkv[part], a[:, c, :], w[:, c, part * N:(part + 1) * N],
                                   start=(r == 0), stop=(r == len(PRODUCTS) - 1))
                    if r == len(PRODUCTS) - 1:
                        mm.then_inc(qkv_done, 1)

            def transpose_xn(t):
                pe.wait_ge(xn_ready, t + 1)
                for c in range(C):
                    mm = pe.transpose(ps_xnT[:, c * P:(c + 1) * P], xn[:, c * P:(c + 1) * P], ident[:, :])
                mm.then_inc(xnT_ready, 1)

            pe.wait_ge(ident_ready, 1)
            pe.wait_ge(couple_in, 16)
            for c in range(C):
                for g in range(C):
                    mm = pe.transpose(psum[:, c, g * P:(g + 1) * P], coupling_nat[:, g, c * P:(c + 1) * P], ident[:, :])
                mm.then_inc(coupT_ready, 1)
            pe.wait_ge(cond_in, 16)
            for c in range(C):
                mm = pe.transpose(psum[:, 4, c * P:(c + 1) * P], q[1][:, c * P:(c + 1) * P], ident[:, :])
            mm.then_inc(condT_done, 1)
            pe.wait_ge(coup_split, C)
            transpose_q(q[0], q_ready, 1)

            def embed(j):
                half, c = divmod(j, C)
                if j == 0:
                    pe.wait_ge(wemb_in, 48)
                    pe.wait_ge(condT_copied, 1)
                w = wemb_nat[0][:, c, :] if half == 0 else wemb_nat[1 + c // 2][:, c % 2, :]
                mm = pe.matmul(psum[:, 5 + half, :], condT[:, c, :], w,
                               start=(c == 0), stop=(c == C - 1))
                if c == C - 1:
                    mm.then_inc(emb_done, 1)

            BEFORE, AFTER = (5, 5, 5, 5), (5, 2, 5, 4)
            FIRST = (BEFORE[2] + AFTER[2] + BEFORE[3] + AFTER[3], 36 - BEFORE[1] - AFTER[1], 0, BEFORE[2] + AFTER[2])
            assert FIRST[0] + BEFORE[0] + AFTER[0] == FIRST[1]

            def step(t, ahead, fill_two, fill_one, fill_embed=False):
                n = t * STAGES
                for s in range(STAGES):
                    couple(n + s)
                    lo, mid, hi = FIRST[s], FIRST[s] + BEFORE[s], FIRST[s] + BEFORE[s] + AFTER[s]
                    fill = fill_two if s < 2 else fill_one
                    of = t - 2 if s < 2 else t - 1
                    if fill:
                        project(of, lo, mid)
                    if fill_embed:
                        embed(2 * s)
                    if s < STAGES - 1:
                        transpose_q(q[s + 1], q_ready, n + s + 2)
                    elif ahead:
                        transpose_q(qraw, combos, COMBOS * (t + 1) + 1)
                    if fill:
                        project(of, mid, hi)
                    if fill_embed:
                        embed(2 * s + 1)
                    if s == 1 and fill_one:
                        transpose_xn(t - 1)

            assert 2 * STAGES == 2 * C
            step(0, True, False, False, fill_embed=True)
            step(1, True, False, True)
            step(2, True, True, True)
            step(3, True, True, True)
            with pe.Fori(2, T // 2 - 1) as m:
                for k in range(2):
                    step(m * 2 + k, True, True, True)
            step(T - 2, True, True, True)
            step(T - 1, False, True, True)
            project(T - 2, FIRST[0], 36)
            transpose_xn(T - 1)
            project(T - 1, 0, 36)

            def transpose_qk(i):
                pe.wait_ge(qkn_ready, i + 1)
                for g in range(G):
                    pe.transpose(ps_QT[:, g * P:(g + 1) * P], qk_norm[:, g * P:(g + 1) * P], ident[:, :])
                for g in range(G):
                    mm = pe.transpose(ps_KT[:, g * P:(g + 1) * P], qk_norm[:, N + g * P:N + (g + 1) * P], ident[:, :])
                mm.then_inc(QKT_ready, 1)

            def scores(i):
                pe.wait_ge(QT_copied, i + 1)
                pe.wait_ge(KT_copied, i + 1)
                for g in range(G):
                    for b in range(2):
                        mm = pe.matmul(ps_S[b * T:(b + 1) * T, g * HG * T:(g + 1) * HG * T],
                                       QT[:, g, b * T:(b + 1) * T],
                                       KT_diag[:, g, b, :, :].rearrange("p h k -> p (h k)"), start=True, stop=True)
                    if g % (G // 2) == G // 2 - 1:
                        mm.then_inc(S_ready, 1)

            def transpose_probs(i):
                pe.wait_ge(probs_ready, 2 * i + 2)
                for hp in range(HP):
                    mm = pe.transpose(ps_PT[:, hp * P:(hp + 1) * P],
                                      probs[:, 2 * hp:2 * hp + 2, :].rearrange("p h k -> p (h k)"), ident[:, :])
                mm.then_inc(PT_ready, 1)

            def attend(i, k, m, first):
                if not first:
                    pe.wait_ge(oT_lo_ready, i)
                pe.wait_ge(PT_copied, i + 1)
                pe.wait_ge(v_loaded[k], 16 * m + 16)
                for hp in range(HP):
                    for b in range(2):
                        mm = pe.matmul(ps_O[b * T:(b + 1) * T, hp * 2 * D:(hp + 1) * 2 * D],
                                       PT[:, hp, b * T:(b + 1) * T], v_in[k][:, b, hp * 2 * D:(hp + 1) * 2 * D],
                                       start=True, stop=True)
                mm.then_inc(O_ready, 1)

            def transpose_o(i):
                pe.wait_ge(o_ready, i + 1)
                for c in range(C):
                    mm = pe.transpose(ps_O[:, c * P:(c + 1) * P], o_row[:, c * P:(c + 1) * P], ident[:, :])
                mm.then_inc(oT_ready, 1)

            def project_out(i, groups, fresh=False):
                for j in groups:
                    a, w = ((oT_hi, wout_hi), (oT_hi, wout_lo), (oT_lo, wout_hi))[j]
                    if j == 0:
                        if not fresh:
                            pe.wait_ge(Y_copied, i)
                        pe.wait_ge(oT_hi_ready, i + 1)
                    if j == 2:
                        pe.wait_ge(oT_lo_ready, i + 1)
                    for c in range(C):
                        mm = pe.matmul(ps_Y, a[:, c, :], w[:, c, :], start=(j == 0 and c == 0), stop=(j == 2 and c == C - 1))
                    if j == 2:
                        mm.then_inc(Y_ready, 1)

            def pair(i, k, m, first=False, fresh=False, score=True, qk=True):
                if score:
                    scores(i + 1)
                attend(i, k, m, first)
                if not first:
                    project_out(i - 1, (0,), fresh)
                if qk:
                    transpose_qk(i + 2)
                if not first:
                    project_out(i - 1, (1, 2))
                transpose_o(i)
                if score:
                    transpose_probs(i + 1)

            pe.wait_ge(qk_copied, T)
            pe.wait_ge(v_ready, T)
            transpose_qk(0)
            scores(0)
            transpose_qk(1)
            transpose_probs(0)
            pe.wait_ge(wout_split, 1)
            pair(0, 0, 0, first=True)
            pair(1, 1, 0, fresh=True)
            with pe.Fori(1, PAIRS // 2 - 1) as m:
                for k in range(2):
                    pair(m * 2 + k, k, m)
            pair(PAIRS - 2, 0, PAIRS // 2 - 1, qk=False)
            pair(PAIRS - 1, 1, PAIRS // 2 - 1, score=False, qk=False)
            project_out(PAIRS - 1, (0, 1, 2))

        @block.scalar
        def _(act):
            def square_q(n, src):
                act.wait_ge(q_ready, n + 1)
                act.activation(ps_cube, src, ACT.Square).then_inc(sq_ready, 1)

            def tanh(n):
                act.wait_ge(qT_ready, n + 1)
                act.activation(tanh_hi[:, :], ps_qT, ACT.Tanh).then_inc(tanh_hi_ready, 1)
                act.activation(ps_tanh, ps_qT, ACT.Tanh).then_inc(tanh_ready, 1)

            def scale_drive(t, first=False):
                act.wait_ge(drive_ready, t + 1)
                if not first:
                    act.wait_ge(pd_ready, 4 * t)
                for n, f in enumerate((BASE[0][DR], BASE[2][DR], BASE[3][DR])):
                    o = act.activation(drive_s[n][:, :], drive[:, :], ACT.Copy, scale=f)
                o.then_inc(drive_s_ready, 1)

            def scale_p(t, lo, hi, first=False):
                if lo == 0:
                    act.wait_ge(combos, COMBOS * t - 2 if not first else 1)
                for s in range(lo, hi):
                    if s == 3 and not first:
                        act.wait_ge(pd_ready, 4 * t)
                    act.activation(p_s[s], p_state[:, :], ACT.Copy, scale=BASE[s][PP]).then_inc(p_s_ready, 1)

            def scale_q1(t, lo, hi, first=False):
                if lo == 1 and not first:
                    act.wait_ge(base_ready, 4 * t)
                for s in range(lo, hi):
                    act.activation(q1_s[s - 1][:, :], q[0][:, :], ACT.Copy, scale=BASE[s][Q1]).then_inc(q1_s_ready, 1)

            def square_x1(t):
                act.wait_ge(x1_ready, t + 1)
                act.activation(sq_dump, x1[:, :], ACT.Square, accum_out=sumsq[:, :]).then_inc(sumsq_ready, 1)

            def copy_qk(t, first=False):
                act.wait_ge(qkv_done, 3 * t + 2)
                if first:
                    act.wait_ge(emb_done, 2)
                else:
                    act.wait_ge(qk_stored, 16 * t)
                act.activation(qk_row[:, :], psum[:, 5:7, :].rearrange("p a n -> p (a n)"), ACT.Copy).then_inc(qk_copied, 1)

            def split_xnT(t):
                act.wait_ge(xnT_ready, t + 1)
                act.activation(xnT_hi[:, :, :].rearrange("p c n -> p (c n)"), ps_xnT, ACT.Copy).then_inc(xnT_hi_ready, 1)

            def copy_v(t, first=False):
                act.wait_ge(qkv_done, 3 * t + 3)
                if not first:
                    act.wait_ge(v_stored, 16 * t)
                else:
                    act.wait_ge(zeros_ready, 1)
                v = ps_qkv[2].rearrange("p (h e d) -> p h e d", e=2, d=D)
                for e in range(2):
                    o = act.activation(v_row[:, e, :].rearrange("p (h e d) -> p h e d", e=2, d=D)[:, :, e, :],
                                       v[:, :, e, :], ACT.Copy)
                o.then_inc(v_ready, 1)

            for c in range(C):
                act.wait_ge(coupT_ready, c + 1)
                act.activation(couple_hi[:, c, :], psum[:, c, :], ACT.Copy).then_inc(coup_hi_ready, 1)
            act.wait_ge(condT_done, 1)
            act.activation(condT[:, :, :].rearrange("p c n -> p (c n)"), psum[:, 4, :], ACT.Copy).then_inc(condT_copied, 1)
            scale_p(0, 0, 3, first=True)
            scale_drive(0, first=True)
            act.wait_ge(coup_split, C)

            def step(t, last, fill_two, fill_one, two_first=False, first=False, between=None):
                n = t * STAGES
                tanh(n)
                square_q(n, q[0][:, :])
                scale_q1(t, 1, 2, first)
                scale_p(t, 3, 4, first)
                if fill_one:
                    square_x1(t - 1)
                scale_q1(t, 2, 3)
                if between:
                    between(0)
                square_q(n + 1, q[1][:, :])
                tanh(n + 1)
                scale_q1(t, 3, 4)
                if between:
                    between(1)
                if fill_two:
                    copy_qk(t - 2, two_first)
                square_q(n + 2, q[2][:, :])
                tanh(n + 2)
                if fill_one:
                    split_xnT(t - 1)
                if between:
                    between(2)
                if fill_two:
                    copy_v(t - 2, two_first)
                square_q(n + 3, q[3][:, :])
                tanh(n + 3)
                if not last:
                    scale_p(t + 1, 0, 1)
                    scale_drive(t + 1)
                    scale_p(t + 1, 1, 3)

            def hi_wqkv(part):
                cols = slice(part * N, (part + 1) * N)
                act.wait_ge(wqkv_in, 16)
                act.activation(wqkv_hi[:, :, cols], wqkv_nat[:, :, cols], ACT.Copy).then_inc(wqkv_hi_ready, 1)

            step(0, False, False, False, first=True)
            step(1, False, False, True, between=hi_wqkv)
            step(2, False, True, True, two_first=True)
            step(3, False, True, True)
            with act.Fori(2, T // 2 - 1) as m:
                for k in range(2):
                    step(m * 2 + k, False, True, True)
            step(T - 2, False, True, True)
            step(T - 1, True, True, True)
            square_x1(T - 1)
            copy_qk(T - 2)
            copy_v(T - 2)
            split_xnT(T - 1)
            act.wait_ge(wout_in, 16)
            act.activation(wout_hi[:, :, :], wout_f32[:, :, :], ACT.Copy).then_inc(wout_hi_ready, 1)
            copy_qk(T - 1)
            copy_v(T - 1)

            def copy_KT(i):
                act.wait_ge(QKT_ready, i + 1)
                for h in range(HG):
                    r = slice(h * D, (h + 1) * D)
                    o = act.activation(KT_diag[r, :, :, h, :], ps_KT[r, :].rearrange("p (g b k) -> p g b k", g=G, b=2), ACT.Copy)
                o.then_inc(KT_copied, 1)

            def scale_QT(i):
                act.activation(QT[:, :, :].rearrange("p g n -> p (g n)"), ps_QT, ACT.Copy, scale=gqk_col[:, 0:1]).then_inc(QT_copied, 1)

            def square_qk(i, k, m, first=False):
                act.wait_ge(qk_loaded[k], 16 * m + 16)
                if not first:
                    act.wait_ge(qk_sum_ready, i)
                act.activation(qk_sq, qk_in[k], ACT.Square).then_inc(qk_sq_ready, 1)

            def exp(i, first=False):
                if not first:
                    act.wait_ge(PT_ready, i)
                    act.wait_ge(sum_ready, 2 * i)
                for half in range(2):
                    h = slice(half * HP, (half + 1) * HP)
                    act.wait_ge(shifted_ready, 2 * i + half + 1)
                    act.activation(probs[:, h, :], shifted[:, h, :], ACT.Exp).then_inc(probs_ready, 1)

            def copy_PT(i):
                act.wait_ge(PT_ready, i + 1)
                act.activation(base_all[:, 0:2 * N], ps_PT, ACT.Copy).then_inc(PT_copied, 1)

            def split_oT(i):
                act.wait_ge(oT_ready, i + 1)
                act.activation(oT_hi[:, :, :].rearrange("p c n -> p (c n)"), ps_O, ACT.Copy).then_inc(oT_hi_ready, 1)

            def copy_Y(i, first=False):
                act.wait_ge(Y_ready, i + 1)
                if not first:
                    act.wait_ge(y_ready, i)
                act.activation(y_copy[:, :], ps_Y, ACT.Copy).then_inc(Y_copied, 1)

            def pair(i, k, m, score=True, qk=True, square=True, first=False, fresh=False):
                if score:
                    exp(i + 1)
                if qk:
                    copy_KT(i + 2)
                    scale_QT(i + 2)
                split_oT(i)
                if score:
                    copy_PT(i + 1)
                if square:
                    square_qk(i + 4, k, m + 2)
                if not first:
                    copy_Y(i - 1, fresh)

            square_qk(0, 0, 0, first=True)
            square_qk(1, 1, 0)
            act.wait_ge(zeros_ready, 2)
            act.wait_ge(gqk_ready, 1)
            copy_KT(0)
            scale_QT(0)
            square_qk(2, 0, 1)
            exp(0, first=True)
            copy_KT(1)
            scale_QT(1)
            copy_PT(0)
            square_qk(3, 1, 1)
            pair(0, 0, 0, first=True)
            pair(1, 1, 0, fresh=True)
            with act.Fori(1, PAIRS // 2 - 2) as m:
                for k in range(2):
                    pair(m * 2 + k, k, m)
            for i in range(PAIRS - 4, PAIRS - 2):
                pair(i, i % 2, i // 2, square=False)
            pair(PAIRS - 2, 0, 0, qk=False, square=False)
            pair(PAIRS - 1, 1, 0, score=False, qk=False, square=False)
            copy_Y(PAIRS - 1)

        @block.vector
        def _(dve):
            stt = dve.scalar_tensor_tensor

            def cube(n, src):
                dve.wait_ge(sq_ready, n + 1)
                stt(ps_cube, ps_cube, -3.0, src, ALU.add, ALU.mult).then_inc(cube_ready, 1)

            def tanh_split(n):
                dve.wait_ge(tanh_ready, n + 1)
                dve.tensor_tensor(tanh_lo[:, :], ps_tanh, tanh_hi[:, :].bitcast(F32), ALU.subtract).then_inc(tanh_lo_ready, 1)

            def b_of(n, s):
                dve.wait_ge(cube_ready, n + 1)
                stt(b_term[:, :], ps_cube, -A_STEP[s] / 3.0, base[s][:, :], ALU.mult, ALU.add).then_inc(b_ready, 1)

            def combine(dst, src, w, add):
                return stt(dst[:, :], src[:, :], w, add[:, :], ALU.mult, ALU.add)

            def next_q(n, s, dst, done):
                dve.wait_ge(b_ready, n + 1)
                dve.wait_ge(coupled, n + 1)
                stt(dst[:, :], ps_couple, A_STEP[s], b_term[:, :], ALU.mult, ALU.add).then_inc(done, 1)

            def norm_x(t):
                dve.wait_ge(rms_ready, t + 1)
                stt(xg[:, :], x1[:, :], rms[:, 0:1], gs_row[:, :], ALU.mult, ALU.mult).then_inc(xg_ready, 1)

            def split_xnT(t):
                dve.wait_ge(xnT_hi_ready, t + 1)
                flat = "p c n -> p (c n)"
                dve.tensor_tensor(xnT_lo[:, :, :].rearrange(flat), ps_xnT, xnT_hi[:, :, :].bitcast(F32).rearrange(flat),
                                  ALU.subtract).then_inc(xnT_lo_ready, 1)

            dve.wait_ge(cond_in, 16)
            dve.tensor_copy(q[0][:, :], q[1][:, :]).then_inc(q_ready, 1)
            dve.tensor_scalar(p_state[:, :], q[1][:, :], -P_SHIFT, None, ALU.add).then_inc(combos, 1)
            dve.wait_ge(rows_in, 48)
            dve.tensor_scalar(bias_row[:, :], bias_row[:, :], -P_SHIFT, None, ALU.add).then_inc(bias_ready, 1)
            for c in range(C):
                dve.wait_ge(coup_hi_ready, c + 1)
                dve.tensor_tensor(couple_lo[:, c, :], psum[:, c, :], couple_hi[:, c, :].bitcast(F32), ALU.subtract).then_inc(coup_split, 1)
            def scale_and_shift():
                dve.wait_ge(emb_done, 2)
                dve.tensor_tensor(shift_row[:, :], psum[:, 6, :], emb_bias[:, N:2 * N], ALU.add).then_inc(emb_read, 1)
                dve.tensor_tensor(emb_bias[:, 0:N], psum[:, 5, :], emb_bias[:, 0:N], ALU.add).then_inc(emb_read, 1)
                dve.wait_ge(emb_read, 2)
                stt(gs_row[:, :], emb_bias[:, 0:N], 1.0, gs_row[:, :], ALU.add, ALU.mult).then_inc(emb_step, 1)
                dve.wait_ge(emb_step, 1)
                dve.tensor_scalar(gs_row[:, :], gs_row[:, :], float(np.sqrt(N)), None, ALU.mult).then_inc(emb_step, 1)
                dve.wait_ge(emb_step, 2)

            def head_gains():
                dve.wait_ge(gcols_in, 16 * 2 * HG)
                dve.tensor_tensor(gqk_col[:, :], gq_col[:, :], gk_col[:, :], ALU.mult).then_inc(gqk_step, 1)
                dve.wait_ge(gqk_step, 1)
                dve.tensor_scalar(gqk_col[:, :], gqk_col[:, :], float(D) * float(D) ** -0.5, None, ALU.mult).then_inc(gqk_ready, 1)

            def lo_wqkv():
                dve.wait_ge(wqkv_hi_ready, 1)
                dve.tensor_tensor(wqkv_lo[:, :, 0:N], wqkv_nat[:, :, 0:N], wqkv_hi[:, :, 0:N].bitcast(F32),
                                  ALU.subtract).then_inc(wqkv_split[0], 1)

            def step(t, fill_one, between=(None,) * STAGES):
                n = t * STAGES
                c0 = COMBOS * t + 1

                dve.wait_ge(combos, c0)
                dve.tensor_scalar(p_sum[:, :], p_state[:, :], P_NEXT[PP], None, ALU.mult).then_inc(combos, 1)
                dve.wait_ge(combos, c0 + 1)
                dve.wait_ge(q_ready, n + 1)
                combine(p_sum, q[0], P_NEXT[Q1], p_sum).then_inc(combos, 1)
                tanh_split(n)
                cube(n, q[0][:, :])
                dve.wait_ge(base_ready, 4 * t + 1)
                b_of(n, 0)
                if between[0]:
                    between[0]()
                next_q(n, 0, q[1], q_ready)

                dve.wait_ge(q_ready, n + 2)
                dve.wait_ge(combos, c0 + 2)
                combine(p_sum, q[1], P_NEXT[Q2], p_sum).then_inc(combos, 1)
                cube(n + 1, q[1][:, :])
                tanh_split(n + 1)
                dve.wait_ge(base_ready, 4 * t + 2)
                b_of(n + 1, 1)
                if fill_one:
                    norm_x(t - 1)
                dve.wait_ge(base_ready, 4 * t + 3)
                combine(base[2], q[1], BASE[2][Q2], base[2]).then_inc(combos, 1)
                if between[1]:
                    between[1]()
                next_q(n + 1, 1, q[2], q_ready)

                dve.wait_ge(combos, c0 + 3)
                dve.wait_ge(q_ready, n + 3)
                combine(p_sum, q[2], P_NEXT[Q3], p_sum).then_inc(combos, 1)
                cube(n + 2, q[2][:, :])
                tanh_split(n + 2)
                dve.wait_ge(combos, c0 + 4)
                b_of(n + 2, 2)
                if fill_one:
                    split_xnT(t - 1)
                dve.wait_ge(base_ready, 4 * t + 4)
                combine(base[3], q[1], BASE[3][Q2], base[3]).then_inc(combos, 1)
                if between[2]:
                    between[2]()
                next_q(n + 2, 2, q[3], q_ready)

                dve.wait_ge(q_ready, n + 4)
                dve.wait_ge(combos, c0 + 5)
                combine(p_sum, q[3], P_NEXT[Q4], p_sum).then_inc(combos, 1)
                cube(n + 3, q[3][:, :])
                dve.wait_ge(combos, c0 + 7)
                dve.wait_ge(p_s_ready, 4 * t + 4)
                dve.tensor_scalar(p_state[:, :], p_sum[:, :], CLAMP - P_SHIFT, -CLAMP - P_SHIFT, ALU.min, ALU.max).then_inc(combos, 1)
                dve.wait_ge(combos, c0 + 6)
                combine(base[3], q[2], BASE[3][Q3], base[3]).then_inc(combos, 1)
                tanh_split(n + 3)
                dve.wait_ge(combos, c0 + 9)
                combine(base[3], q[3], BASE[3][Q4], base[3]).then_inc(combos, 1)
                dve.wait_ge(combos, c0 + 10)
                b_of(n + 3, 3)
                if between[3]:
                    between[3]()
                next_q(n + 3, 3, qraw, combos)
                dve.wait_ge(combos, c0 + 11)
                if fill_one:
                    dve.wait_ge(x1_ready, t)
                dve.tensor_scalar(q[0][:, :], qraw[:, :], CLAMP, -CLAMP, ALU.min, ALU.max).then_inc(q_ready, 1)

            step(0, False, between=(head_gains, None, None, None))
            step(1, True, between=(scale_and_shift, lo_wqkv, None, None))
            with dve.Fori(1, T // 2) as m:
                for k in range(2):
                    step(m * 2 + k, True)
            norm_x(T - 1)
            split_xnT(T - 1)
            dve.wait_ge(wout_hi_ready, 1)
            dve.tensor_tensor(wout_lo[:, :, :], wout_f32[:, :, :], wout_hi[:, :, :].bitcast(F32), ALU.subtract).then_inc(wout_split, 1)

            def sum_qk(i):
                dve.wait_ge(qk_sq_ready, i + 1)
                dve.tensor_reduce(head_sum[:, :], qk_sq.rearrange("p (h d) -> p h d", d=D), AX.X, ALU.add).then_inc(qk_sum_ready, 1)

            def head_root(i, lo=0, hi=ROOT_OPS):
                r0 = ROOT_OPS * i
                for j in range(lo, hi):
                    if j == 0:
                        dve.wait_ge(qk_sum_ready, i + 1)
                        o = dve.tensor_scalar(head_eps[:, :], head_sum[:, :], D * EPS, None, ALU.add)
                    elif j == 1:
                        o = dve.tensor_scalar(head_half[:, :], head_sum[:, :], D * EPS, -0.5, ALU.add, ALU.mult)
                    elif j == 2:
                        dve.wait_ge(qk_root, r0 + 1)
                        o = dve.tensor_scalar(head_tmp[:, :].bitcast(I32), head_eps[:, :].bitcast(I32), 1, None,
                                              ALU.logical_shift_right)
                    elif j == 3:
                        dve.wait_ge(qk_root, r0 + 3)
                        if not (isinstance(i, int) and i == 0):
                            dve.wait_ge(qkn_ready, i)
                        o = dve.tensor_scalar(head_rms[:, :].bitcast(I32), head_tmp[:, :].bitcast(I32), -1.0,
                                              float(0x5F3759DF), ALU.mult, ALU.add)
                    else:
                        dve.wait_ge(qk_root, r0 + j)
                        if j % 3 == 1:
                            o = dve.tensor_tensor(head_tmp[:, :], head_rms[:, :], head_rms[:, :], ALU.mult)
                        elif j % 3 == 2:
                            o = dve.tensor_tensor(head_tmp[:, :], head_tmp[:, :], head_half[:, :], ALU.mult)
                        else:
                            o = stt(head_rms[:, :], head_tmp[:, :], 1.5, head_rms[:, :], ALU.add, ALU.mult)
                    o.then_inc(qk_root, 1)

            S = ps_S.rearrange("p (h k) -> p h k", k=T)
            halves = [slice(half * HP, (half + 1) * HP) for half in range(2)]

            def row_max(i, half):
                h = halves[half]
                dve.wait_ge(S_ready, 2 * i + half + 1)
                dve.tensor_reduce(neg_max[:, h], S[:, h, :], AX.X, ALU.max, negate=True).then_inc(max_ready, 1)

            def shift(i, half):
                h = halves[half]
                dve.wait_ge(max_ready, 2 * i + half + 1)
                dve.tensor_tensor(shifted[:, h, :], S[:, h, :], neg_max[:, h].unsqueeze(2).to_broadcast([P, HP, T]),
                                  ALU.add).then_inc(shifted_ready, 1)

            def sum_probs(i, half):
                h = halves[half]
                dve.wait_ge(probs_ready, 2 * i + half + 1)
                dve.tensor_reduce(row_sum[:, h], probs[:, h, :], AX.X, ALU.add).then_inc(sum_ready, 1)

            def invert_sum(i):
                dve.wait_ge(sum_ready, 2 * i + 2)
                dve.reciprocal(row_rcp[:, :], row_sum[:, :]).then_inc(rcp_ready, 1)

            def norm_o(i, first=False):
                dve.wait_ge(rcp_ready, i + 1)
                dve.wait_ge(O_ready, i + 1)
                if not first:
                    dve.wait_ge(resid_ready, i)
                dve.tensor_tensor(o_row[:, :].rearrange("p (h d) -> p h d", d=D), ps_O.rearrange("p (h d) -> p h d", d=D),
                                  row_rcp[:, :].unsqueeze(2).to_broadcast([P, HEADS, D]), ALU.mult).then_inc(o_ready, 1)

            def split_oT(i):
                dve.wait_ge(oT_hi_ready, i + 1)
                flat = "p c n -> p (c n)"
                dve.tensor_tensor(oT_lo[:, :, :].rearrange(flat), ps_O, oT_hi[:, :, :].bitcast(F32).rearrange(flat),
                                  ALU.subtract).then_inc(oT_lo_ready, 1)

            def pair(i, score=True, root=True, first=False):
                def small(lo, hi):
                    if root:
                        head_root(i + 3, lo, hi)

                if score:
                    row_max(i + 1, 0)
                    row_max(i + 1, 1)
                    shift(i + 1, 0)
                    shift(i + 1, 1)
                if root:
                    sum_qk(i + 3)
                norm_o(i, first)
                small(0, 3)
                if score:
                    sum_probs(i + 1, 0)
                    small(3, 4)
                    sum_probs(i + 1, 1)
                    small(4, 5)
                    invert_sum(i + 1)
                small(5, 8)
                split_oT(i)
                small(8, ROOT_OPS)

            sum_qk(0)
            head_root(0)
            sum_qk(1)
            head_root(1)
            for half in range(2):
                row_max(0, half)
                shift(0, half)
            sum_qk(2)
            head_root(2)
            sum_probs(0, 0)
            sum_probs(0, 1)
            invert_sum(0)
            pair(0, first=True)
            with dve.Fori(0, (PAIRS - 4) // UNROLL) as m:
                for k in range(UNROLL):
                    pair(m * UNROLL + (k + 1))
            pair(PAIRS - 3, root=False)
            pair(PAIRS - 2, root=False)
            pair(PAIRS - 1, score=False, root=False)

        @block.gpsimd
        def _(pool):
            def add(dst, a, b):
                return pool.tensor_tensor(dst[:, :], a[:, :], b[:, :], ALU.add)

            def add_p(t, s, first=False):
                if s == 0:
                    pool.wait_ge(drive_s_ready, t + 1)
                if s == 3 and not first:
                    pool.wait_ge(b_ready, 4 * t)
                pool.wait_ge(p_s_ready, 4 * t + s + 1)
                pool.tensor_tensor(base[s], drive_s[(0, 0, 1, 2)[s]][:, :], p_s[s], ALU.add).then_inc(pd_ready, 1)

            def add_q1(t, s):
                if s == 0:
                    pool.wait_ge(q_ready, 4 * t + 1)
                    src = q[0]
                else:
                    pool.wait_ge(q1_s_ready, 3 * t + s)
                    src = q1_s[s - 1]
                pool.wait_ge(pd_ready, 4 * t + s + 1)
                add(base[s], base[s], src).then_inc(base_ready, 1)

            def make_drive(t, k, m, first=False):
                pool.wait_ge(x_loaded[k], 16 * m + 16)
                if not first:
                    pool.wait_ge(drive_s_ready, t)
                add(drive, x_in[k], bias_row).then_inc(drive_ready, 1)

            def make_x1(t, k, first=False):
                pool.wait_ge(q_ready, 4 * t + 5)
                if not first:
                    pool.wait_ge(x1_stored, 16 * t)
                add(x1, x_in[k], q[0]).then_inc(x1_ready, 1)

            def rms_x(t, first=False):
                pool.wait_ge(sumsq_ready, t + 1)
                if first:
                    pool.wait_ge(half_ready, 2)
                pool.tensor_tensor(sumsq_eps[:, :], sumsq[:, :], eps_col[:, :], ALU.add).then_inc(sumsq_eps_ready, 1)
                pool.wait_ge(sumsq_eps_ready, t + 1)
                pool.tensor_tensor(rms[:, :], sumsq_eps[:, :], minus_half[:, :], ALU.pow).then_inc(rms_ready, 1)

            def shift_x(t, first=False):
                pool.wait_ge(xg_ready, t + 1)
                if not first:
                    pool.wait_ge(xnT_ready, t)
                add(xn, xg, shift_row).then_inc(xn_ready, 1)

            pool.memset(ident[:, :], 0.0).then_inc(ident_zero, 1)
            pool.wait_ge(ident_zero, 1)
            pool.affine_select(out=ident[:, :], in_=ident[:, :], compare_op=ALU.not_equal, fill=1.0,
                               base=0, pattern=[[-1, P]], channel_multiplier=1).then_inc(ident_ready, 1)
            pool.memset(minus_half[:, :], -0.5).then_inc(half_ready, 1)
            pool.memset(eps_col[:, :], N * EPS).then_inc(half_ready, 1)
            pool.wait_ge(bias_ready, 1)
            make_drive(0, 0, 0, first=True)
            add_p(0, 0)
            add_p(0, 1)

            def lo_wqkv(part):
                cols = slice(part * N, (part + 1) * N)
                pool.wait_ge(wqkv_hi_ready, part + 1)
                pool.tensor_tensor(wqkv_lo[:, :, cols], wqkv_nat[:, :, cols], wqkv_hi[:, :, cols].bitcast(F32),
                                   ALU.subtract).then_inc(wqkv_split[part], 1)

            def step(t, k, m, last, fill_one, x_first=False):
                add_q1(t, 0)
                if fill_one:
                    make_x1(t - 1, 1 - k, x_first)
                add_q1(t, 1)
                if fill_one:
                    rms_x(t - 1, x_first)
                add_p(t, 2)
                add_q1(t, 2)
                if fill_one:
                    if x_first:
                        pool.wait_ge(emb_read, 2)
                    shift_x(t - 1, x_first)
                add_p(t, 3, first=not fill_one)
                add_q1(t, 3)
                if not last:
                    make_drive(t + 1, 1 - k, m + k)
                    if x_first:
                        lo_wqkv(1)
                        lo_wqkv(2)
                    add_p(t + 1, 0)
                    add_p(t + 1, 1)

            step(0, 0, 0, False, False)
            pool.wait_ge(emb_done, 2)
            pool.memset(v_row[:, :, :], 0.0).then_inc(zeros_ready, 1)
            step(1, 1, 0, False, True, x_first=True)
            with pool.Fori(1, T // 2 - 1) as m:
                for k in range(2):
                    step(m * 2 + k, k, m, False, True)
            step(T - 2, 0, T // 2 - 1, False, True)
            step(T - 1, 1, T // 2 - 1, True, True)
            make_x1(T - 1, 1)
            rms_x(T - 1)
            shift_x(T - 1)
            for part in range(3):
                pool.wait_ge(wqkv_split[part], 1)
            pool.memset(KT_diag[:, :, :, :, :], 0.0).then_inc(zeros_ready, 1)

            def residual(i, k, m, fresh=False):
                pool.wait_ge(o_ready, i + 1)
                if not fresh:
                    pool.wait_ge(y_ready, i - 1)
                pool.wait_ge(x1_loaded[k], 16 * m + 16)
                add(resid[k], o_row, x1_in[k]).then_inc(resid_ready, 1)

            def add_y(i, k, m, fresh=False):
                pool.wait_ge(resid_ready, i + 1)
                pool.wait_ge(Y_copied, i + 1)
                if not fresh:
                    pool.wait_ge(y_stored[k], 16 * m)
                pool.tensor_tensor(y_row[k], resid[k][:, :], y_copy[:, :], ALU.add).then_inc(y_ready, 1)

            def norm_qk(i, k, first=False):
                pool.wait_ge(qk_root, ROOT_OPS * (i + 1))
                if not first:
                    pool.wait_ge(QKT_ready, i)
                pool.tensor_tensor(qk_norm[:, :].rearrange("p (h d) -> p h d", d=D), qk_in[k].rearrange("p (h d) -> p h d", d=D),
                                   head_rms[:, :].unsqueeze(2).to_broadcast([P, 2 * HEADS, D]), ALU.mult).then_inc(qkn_ready, 1)

            norm_qk(0, 0, first=True)
            norm_qk(1, 1)
            norm_qk(2, 0)

            def pair(i, k, m, fresh=False):
                residual(i, k, m, fresh=isinstance(i, int) and i == 1)
                norm_qk(i + 3, 1 - k)
                add_y(i - 1, 1 - k, m - 1 + k, fresh)

            residual(0, 0, 0, fresh=True)
            norm_qk(3, 1)
            pair(1, 1, 0, fresh=True)
            pair(2, 0, 1, fresh=True)
            pair(3, 1, 1)
            with pool.Fori(2, PAIRS // 2 - 2) as m:
                for k in range(2):
                    pair(m * 2 + k, k, m)
            pair(PAIRS - 4, 0, PAIRS // 2 - 2)
            for i in range(PAIRS - 3, PAIRS):
                residual(i, i % 2, i // 2)
                add_y(i - 1, (i - 1) % 2, (i - 1) // 2)
            add_y(PAIRS - 1, 1, PAIRS // 2 - 1)


_INS = ["x", "cond_2048", "L0_cond_coupling", "L0_cond_bias", "L1_cond_W_emb", "L1_cond_b_emb", "L1_cond_g_norm",
        "L1_cond_W_qkv", "L1_cond_g_q", "L1_cond_g_k", "L1_cond_W_out"]


def kernel(**inputs):
    import numpy as _np
    import concourse.bacc as _bacc
    from concourse import mybir as _mybir
    from concourse.bass_utils import run_bass_kernel_spmd as _run

    nc = _bacc.Bacc("TRN2", target_bir_lowering=False, num_devices=1)
    arrays, args = {}, []
    for name in _INS:
        a = _np.ascontiguousarray(inputs[name])
        arrays[f"in_{name}"] = a
        args.append(nc.dram_tensor(f"in_{name}", a.shape, _mybir.dt.from_np(a.dtype), kind="ExternalInput").ap())
    shape = inputs["x"].shape
    args.append(nc.dram_tensor("out_0", shape, _mybir.dt.float32, kind="ExternalOutput").ap())
    fhn_attention_kernel(nc, *args)
    r = _run(nc, [arrays], core_ids=[0])
    return r.results[0]["out_0"]
```
